# Optimizing a Trainium2 kernel written in Bass

```python
import numpy as np
import jax
import jax.numpy as jnp

def _softmax(x, axis=-1):
    return jax.nn.softmax(x, axis=axis)

def _gelu(x):
    return jax.nn.gelu(x, approximate=True)

def _silu(x):
    return jax.nn.silu(x)

def _sigmoid(x):
    return jax.nn.sigmoid(x)

def _layernorm(x, axis=-1, eps=1e-05):
    m = jnp.mean(x, axis=axis, keepdims=True)
    v = jnp.var(x, axis=axis, keepdims=True)
    return (x - m) / jnp.sqrt(v + eps)

def _scatter_add(tgt, idx, src, axis=0):
    return tgt.at[idx].add(src)

def _segment_sum(src, seg, n):
    return jax.ops.segment_sum(src, seg, n)
kernel_name = 'mk_gps_d2_gnn_r8_ce0838'

def setup_inputs(seed: int=0):
    np.random.seed(seed)
    _w = jnp.asarray

    def _rec_inputs():
        import jax
        import jax.numpy as jnp
        _gk = jax.random.key(seed)
        x = -0.0001126 + 1 * jax.random.normal(jax.random.fold_in(_gk, 1), (1250, 768), jnp.float32)
        src = jax.random.randint(jax.random.fold_in(_gk, 2), (40000,), 0, 1250, jnp.int32)
        dst = jnp.minimum((1250 * jax.random.uniform(jax.random.fold_in(_gk, 3), (40000,)) ** 2.0).astype(jnp.int32), 9999)
        _o = jnp.argsort(dst, stable=True)
        src = src[_o]
        dst = dst[_o]
        return (x, src, dst)
    x, src, dst = _rec_inputs()

    def _L0_gnn_setup():
        import jax, jax.numpy as jnp
        import numpy as np
        N_NODES = 1250
        N_EDGES = 20000
        NEG_SLOPE = 0.2

        def _gat_layer(x, src, dst, W, a_src, a_dst, bias, concat):
            N = x.shape[0]
            H, C = a_src.shape
            h = (x @ W).reshape(N, H, C)
            al_s = jnp.einsum('nhc,hc->nh', h, a_src)
            al_d = jnp.einsum('nhc,hc->nh', h, a_dst)
            e = jax.nn.leaky_relu(al_s[src] + al_d[dst], NEG_SLOPE)
            m = jax.ops.segment_max(e, dst, num_segments=N)
            ex = jnp.exp(e - m[dst])
            denom = jax.ops.segment_sum(ex, dst, num_segments=N)
            alpha = ex / (denom[dst] + 1e-16)
            msg = h[src] * alpha[:, :, None]
            out = jax.ops.segment_sum(msg, dst, num_segments=N)
            out = out.reshape(N, H * C) if concat else out.mean(axis=1)
            return out + bias
        key = jax.random.key(seed)
        ks = jax.random.split(key, 10)
        in_dim, hid, out_dim, heads = (768, 512, 768, 4)
        x = jax.random.normal(ks[0], (N_NODES, in_dim), dtype=jnp.float32)
        edge_index = jax.random.randint(ks[1], (2, N_EDGES), 0, N_NODES, dtype=jnp.int64)
        g = lambda k, shape, fan: jax.random.normal(k, shape, jnp.float32) / np.sqrt(fan)
        return {'x': x, 'edge_index': edge_index, 'W1': g(ks[2], (in_dim, heads * hid), in_dim), 'att_src1': g(ks[3], (heads, hid), hid), 'att_dst1': g(ks[4], (heads, hid), hid), 'b1': jnp.zeros((heads * hid,), jnp.float32), 'W2': g(ks[5], (heads * hid, out_dim), heads * hid), 'att_src2': g(ks[6], (1, out_dim), out_dim), 'att_dst2': g(ks[7], (1, out_dim), out_dim), 'b2': jnp.zeros((out_dim,), jnp.float32)}
    _L0_gnn_all = _L0_gnn_setup()
    _L0_gnn_in = {k: v for k, v in _L0_gnn_all.items() if k in ('W1', 'att_src1', 'att_dst1', 'b1', 'W2', 'att_src2', 'att_dst2', 'b2')}
    del _L0_gnn_all

    def _L0_mix_setup():
        import jax, jax.numpy as jnp
        import numpy as np
        B, N, C, H = (8, 512, 768, 12)
        DH = C // H
        EPS = 1e-06

        def _reference_tuple_inner(x, qkv_w, proj_w, proj_b):
            b, n, c = x.shape
            qkv = x @ qkv_w.T
            qkv = qkv.reshape(b, n, 3, H, DH).transpose(2, 0, 3, 1, 4)
            q, k, v = (qkv[0], qkv[1], qkv[2])
            q = jax.nn.elu(q) + 1.0
            k = jax.nn.elu(k) + 1.0
            kv = jnp.einsum('bhnd,bhne->bhde', k, v)
            ksum = k.sum(axis=-2)
            z = 1.0 / (jnp.einsum('bhnd,bhd->bhn', q, ksum) + EPS)
            out = jnp.einsum('bhnd,bhde->bhne', q, kv) * z[..., None]
            out = out.transpose(0, 2, 1, 3).reshape(b, n, c)
            out = out @ proj_w.T + proj_b
            return (out, kv)
        key = jax.random.key(seed)
        k1, k2, k3, k4 = jax.random.split(key, 4)
        x = jax.random.normal(k1, (B, N, C), dtype=jnp.float32)
        qkv_w = jax.random.normal(k2, (3 * C, C), dtype=jnp.float32) * (1.0 / np.sqrt(C))
        proj_w = jax.random.normal(k3, (C, C), dtype=jnp.float32) * (1.0 / np.sqrt(C))
        proj_b = jax.random.normal(k4, (C,), dtype=jnp.float32) * 0.01
        return {'x': x, 'qkv_w': qkv_w, 'proj_w': proj_w, 'proj_b': proj_b}
    _L0_mix_all = _L0_mix_setup()
    _L0_mix_in = {k: v for k, v in _L0_mix_all.items() if k in ('qkv_w', 'proj_w', 'proj_b')}
    del _L0_mix_all

    def _L0_ffn_setup():
        import jax, jax.numpy as jnp
        import numpy as np
        DEPTH = 11

        def _fff_forward(inputs, weights_in, weights_out, depth=DEPTH):
            B, S, _ = inputs.shape
            n_nodes = weights_in.shape[0]
            max_index = n_nodes - 1
            all_logits = jnp.einsum('bsd,nd->bsn', inputs, weights_in)

            def step(prev_idx, _):
                sel = jnp.clip(prev_idx, 0, max_index)
                logits = jnp.take_along_axis(all_logits, sel[..., None], axis=-1)[..., 0]
                new_idx = jnp.clip(2 * sel + 1 + (logits > 0).astype(sel.dtype), 0, max_index)
                return (new_idx, (logits, new_idx))
            idx0 = jnp.zeros((B, S), dtype=jnp.int32)
            _, (logits_seq, idx_seq) = jax.lax.scan(step, idx0, None, length=depth - 1)
            logits = jnp.concatenate([jnp.zeros((1, B, S), all_logits.dtype), logits_seq], axis=0)
            node_idx = jnp.concatenate([idx0[None], idx_seq], axis=0)
            act = jax.nn.gelu(logits, approximate=False)
            onehot = jax.nn.one_hot(node_idx, n_nodes, dtype=act.dtype)
            coeff = jnp.einsum('dbs,dbsn->bsn', act, onehot)
            return jnp.einsum('bsn,nd->bsd', coeff, weights_out)
        key = jax.random.key(seed)
        k1, k2, k3 = jax.random.split(key, 3)
        B, S, D = (4, 512, 768)
        n_nodes = 2 * DEPTH - 1
        return {'inputs': jax.random.normal(k1, (B, S, D), dtype=jnp.float32), 'weights_in': jax.random.normal(k2, (n_nodes, D), dtype=jnp.float32), 'weights_out': jax.random.normal(k3, (n_nodes, D), dtype=jnp.float32)}
    _L0_ffn_all = _L0_ffn_setup()
    _L0_ffn_in = {k: v for k, v in _L0_ffn_all.items() if k in ('weights_in', 'weights_out')}
    del _L0_ffn_all

    def _L1_gnn_setup():
        import jax, jax.numpy as jnp
        import numpy as np
        N_NODES = 1250
        key = jax.random.key(seed)
        k1, k2, k3 = jax.random.split(key, 3)
        x = jax.random.normal(k1, (N_NODES, 768), dtype=jnp.float32)
        edge_index = jax.random.randint(k2, (2, 12500), 0, N_NODES, dtype=jnp.int32)
        W = jax.random.normal(k3, (768, 768), dtype=jnp.float32) * (1.0 / np.sqrt(768))
        b = jnp.zeros((768,), dtype=jnp.float32)
        return {'x': x, 'edge_index': edge_index, 'W': W, 'b': b}
    _L1_gnn_all = _L1_gnn_setup()
    _L1_gnn_in = {k: v for k, v in _L1_gnn_all.items() if k in ('W', 'b')}
    del _L1_gnn_all

    def _L1_mix_setup():
        import jax, jax.numpy as jnp
        import numpy as np
        DIM = 768
        HEADS = 12
        DH = DIM // HEADS
        M = 256
        EPS = 0.0001

        def softmax_kernel(data, proj, is_query):
            data_normalizer = data.shape[-1] ** (-0.25)
            ratio = proj.shape[0] ** (-0.5)
            data_dash = jnp.einsum('bhsd,md->bhsm', data_normalizer * data, proj)
            diag = 0.5 * data_normalizer ** 2 * jnp.sum(data * data, axis=-1, keepdims=True)
            if is_query:
                stab = jnp.max(data_dash, axis=-1, keepdims=True)
            else:
                stab = jnp.max(data_dash, axis=(-2, -1), keepdims=True)
            stab = jax.lax.stop_gradient(stab)
            return ratio * (jnp.exp(data_dash - diag - stab) + EPS)
        key = jax.random.key(seed)
        kx, kq, kk, kv, ko, kp = jax.random.split(key, 6)
        B, S = (8, 512)
        w_scale = DIM ** (-0.5)
        return {'x': jax.random.normal(kx, (B, S, DIM), jnp.float32), 'Wq': jax.random.normal(kq, (DIM, DIM), jnp.float32) * w_scale, 'Wk': jax.random.normal(kk, (DIM, DIM), jnp.float32) * w_scale, 'Wv': jax.random.normal(kv, (DIM, DIM), jnp.float32) * w_scale, 'Wo': jax.random.normal(ko, (DIM, DIM), jnp.float32) * w_scale, 'proj': jax.random.normal(kp, (M, DH), jnp.float32)}
    _L1_mix_all = _L1_mix_setup()
    _L1_mix_in = {k: v for k, v in _L1_mix_all.items() if k in ('Wq', 'Wk', 'Wv', 'Wo', 'proj')}
    del _L1_mix_all

    def _L1_ffn_setup():
        import jax, jax.numpy as jnp
        import numpy as np
        import math
        N_HEAD = 12
        N_EXP = 8
        TOP_K = 2
        EVAL_CAPACITY = 1.0
        MIN_CAPACITY = 4
        EPS = 1e-05

        def layer_norm(x, w):
            mu = jnp.mean(x, axis=-1, keepdims=True)
            var = jnp.var(x, axis=-1, keepdims=True)
            return (x - mu) / jnp.sqrt(var + EPS) * w

        def attention(x, c_attn_w, c_proj_w):
            B, T, C = x.shape
            H, D = (N_HEAD, C // N_HEAD)
            qkv = x @ c_attn_w.T
            q, k, v = jnp.split(qkv, 3, axis=-1)
            q = q.reshape(B, T, H, D).transpose(0, 2, 1, 3)
            k = k.reshape(B, T, H, D).transpose(0, 2, 1, 3)
            v = v.reshape(B, T, H, D).transpose(0, 2, 1, 3)
            scores = jnp.einsum('bhqd,bhkd->bhqk', q, k) * (1.0 / math.sqrt(D))
            causal = jnp.tril(jnp.ones((T, T), dtype=bool))
            scores = jnp.where(causal, scores, -jnp.inf)
            att = jax.nn.softmax(scores, axis=-1)
            y = jnp.einsum('bhqk,bhkd->bhqd', att, v)
            y = y.transpose(0, 2, 1, 3).reshape(B, T, C)
            return y @ c_proj_w.T

        def get_capacity(num_tokens):
            cap = int(math.floor(TOP_K * EVAL_CAPACITY * num_tokens / N_EXP))
            cap += cap % 2
            return max(cap, MIN_CAPACITY)

        def moe(x_flat, w_g, c_fc, c_proj_e):
            n_tok, C = x_flat.shape
            logits = x_flat @ w_g.T
            top_vals, top_idx = jax.lax.top_k(logits, TOP_K)
            rows = jnp.arange(n_tok)[:, None]
            masked = jnp.full_like(logits, -jnp.inf).at[rows, top_idx].set(top_vals)
            probs = jax.nn.softmax(masked, axis=-1)
            cap = get_capacity(n_tok)
            flat_e = top_idx.reshape(-1)
            onehot = jax.nn.one_hot(flat_e, N_EXP, dtype=jnp.int32)
            pos = jnp.cumsum(onehot, axis=0) - onehot
            slot = jnp.take_along_axis(pos, flat_e[:, None], axis=1)[:, 0]
            valid = slot < cap
            tok = jnp.repeat(jnp.arange(n_tok), TOP_K)
            slot_c = jnp.where(valid, slot, cap)
            sec = jnp.zeros((n_tok, N_EXP, cap + 1), dtype=x_flat.dtype)
            sec = sec.at[tok, flat_e, slot_c].set(1.0)[:, :, :cap]
            w_tok = probs[tok, flat_e]
            cb = jnp.zeros((n_tok, N_EXP, cap + 1), dtype=x_flat.dtype)
            cb = cb.at[tok, flat_e, slot_c].set(w_tok)[:, :, :cap]
            dispatched = jnp.einsum('tec,td->ecd', sec, x_flat)
            h = jax.nn.gelu(jnp.einsum('ecd,edh->ech', dispatched, c_fc), approximate=False)
            out = jnp.einsum('ech,ehd->ecd', h, c_proj_e)
            return jnp.einsum('tec,ecd->td', cb, out)
        key = jax.random.key(seed)
        ks = jax.random.split(key, 7)
        B, T, C = (2, 256, 768)
        std = 0.02
        return {'x': jax.random.normal(ks[0], (B, T, C), dtype=jnp.float32), 'ln1_w': jnp.ones((C,), dtype=jnp.float32), 'ln2_w': jnp.ones((C,), dtype=jnp.float32), 'c_attn_w': jax.random.normal(ks[1], (3 * C, C), dtype=jnp.float32) * std, 'c_proj_w': jax.random.normal(ks[2], (C, C), dtype=jnp.float32) * std, 'w_g': jax.random.normal(ks[3], (N_EXP, C), dtype=jnp.float32) * std, 'c_fc': jax.random.normal(ks[4], (N_EXP, C, 4 * C), dtype=jnp.float32) * std, 'c_proj_e': jax.random.normal(ks[5], (N_EXP, 4 * C, C), dtype=jnp.float32) * std}
    _L1_ffn_all = _L1_ffn_setup()
    _L1_ffn_in = {k: v for k, v in _L1_ffn_all.items() if k in ('ln1_w', 'ln2_w', 'c_attn_w', 'c_proj_w', 'w_g', 'c_fc', 'c_proj_e')}
    del _L1_ffn_all
    return {'x': x, 'src': src, 'dst': dst, 'L0_gnn_W1': _L0_gnn_in['W1'], 'L0_gnn_att_src1': _L0_gnn_in['att_src1'], 'L0_gnn_att_dst1': _L0_gnn_in['att_dst1'], 'L0_gnn_b1': _L0_gnn_in['b1'], 'L0_gnn_W2': _L0_gnn_in['W2'], 'L0_gnn_att_src2': _L0_gnn_in['att_src2'], 'L0_gnn_att_dst2': _L0_gnn_in['att_dst2'], 'L0_gnn_b2': _L0_gnn_in['b2'], 'L0_mix_qkv_w': _L0_mix_in['qkv_w'], 'L0_mix_proj_w': _L0_mix_in['proj_w'], 'L0_mix_proj_b': _L0_mix_in['proj_b'], 'L0_ffn_weights_in': _L0_ffn_in['weights_in'], 'L0_ffn_weights_out': _L0_ffn_in['weights_out'], 'L1_gnn_W': _L1_gnn_in['W'], 'L1_gnn_b': _L1_gnn_in['b'], 'L1_mix_Wq': _L1_mix_in['Wq'], 'L1_mix_Wk': _L1_mix_in['Wk'], 'L1_mix_Wv': _L1_mix_in['Wv'], 'L1_mix_Wo': _L1_mix_in['Wo'], 'L1_mix_proj': _L1_mix_in['proj'], 'L1_ffn_ln1_w': _L1_ffn_in['ln1_w'], 'L1_ffn_ln2_w': _L1_ffn_in['ln2_w'], 'L1_ffn_c_attn_w': _L1_ffn_in['c_attn_w'], 'L1_ffn_c_proj_w': _L1_ffn_in['c_proj_w'], 'L1_ffn_w_g': _L1_ffn_in['w_g'], 'L1_ffn_c_fc': _L1_ffn_in['c_fc'], 'L1_ffn_c_proj_e': _L1_ffn_in['c_proj_e']}

def reference(x, src, dst, L0_gnn_W1, L0_gnn_att_src1, L0_gnn_att_dst1, L0_gnn_b1, L0_gnn_W2, L0_gnn_att_src2, L0_gnn_att_dst2, L0_gnn_b2, L0_mix_qkv_w, L0_mix_proj_w, L0_mix_proj_b, L0_ffn_weights_in, L0_ffn_weights_out, L1_gnn_W, L1_gnn_b, L1_mix_Wq, L1_mix_Wk, L1_mix_Wv, L1_mix_Wo, L1_mix_proj, L1_ffn_ln1_w, L1_ffn_ln2_w, L1_ffn_c_attn_w, L1_ffn_c_proj_w, L1_ffn_w_g, L1_ffn_c_fc, L1_ffn_c_proj_e):
    import jax
    import jax.numpy as jnp

    def _L0_gnn_ref(x, edge_index, W1, att_src1, att_dst1, b1, W2, att_src2, att_dst2, b2):
        import jax, jax.numpy as jnp
        import numpy as np
        N_NODES = 1250
        N_EDGES = 20000
        NEG_SLOPE = 0.2

        def _gat_layer(x, src, dst, W, a_src, a_dst, bias, concat):
            N = x.shape[0]
            H, C = a_src.shape
            h = (x @ W).reshape(N, H, C)
            al_s = jnp.einsum('nhc,hc->nh', h, a_src)
            al_d = jnp.einsum('nhc,hc->nh', h, a_dst)
            e = jax.nn.leaky_relu(al_s[src] + al_d[dst], NEG_SLOPE)
            m = jax.ops.segment_max(e, dst, num_segments=N)
            ex = jnp.exp(e - m[dst])
            denom = jax.ops.segment_sum(ex, dst, num_segments=N)
            alpha = ex / (denom[dst] + 1e-16)
            msg = h[src] * alpha[:, :, None]
            out = jax.ops.segment_sum(msg, dst, num_segments=N)
            out = out.reshape(N, H * C) if concat else out.mean(axis=1)
            return out + bias
        N = x.shape[0]
        loops = jnp.arange(N, dtype=edge_index.dtype)
        src = jnp.concatenate([edge_index[0], loops])
        dst = jnp.concatenate([edge_index[1], loops])
        h = jax.nn.elu(_gat_layer(x, src, dst, W1, att_src1, att_dst1, b1, concat=True))
        out = _gat_layer(h, src, dst, W2, att_src2, att_dst2, b2, concat=False)
        return out

    def _L0_mix_ref(x, qkv_w, proj_w, proj_b):
        import jax, jax.numpy as jnp
        import numpy as np
        B, N, C, H = (8, 512, 768, 12)
        DH = C // H
        EPS = 1e-06

        def _reference_tuple_inner(x, qkv_w, proj_w, proj_b):
            b, n, c = x.shape
            qkv = x @ qkv_w.T
            qkv = qkv.reshape(b, n, 3, H, DH).transpose(2, 0, 3, 1, 4)
            q, k, v = (qkv[0], qkv[1], qkv[2])
            q = jax.nn.elu(q) + 1.0
            k = jax.nn.elu(k) + 1.0
            kv = jnp.einsum('bhnd,bhne->bhde', k, v)
            ksum = k.sum(axis=-2)
            z = 1.0 / (jnp.einsum('bhnd,bhd->bhn', q, ksum) + EPS)
            out = jnp.einsum('bhnd,bhde->bhne', q, kv) * z[..., None]
            out = out.transpose(0, 2, 1, 3).reshape(b, n, c)
            out = out @ proj_w.T + proj_b
            return (out, kv)
        return _reference_tuple_inner(x, qkv_w, proj_w, proj_b)[0]

    def _L0_ffn_ref(inputs, weights_in, weights_out):
        import jax, jax.numpy as jnp
        import numpy as np
        DEPTH = 11

        def _fff_forward(inputs, weights_in, weights_out, depth=DEPTH):
            B, S, _ = inputs.shape
            n_nodes = weights_in.shape[0]
            max_index = n_nodes - 1
            all_logits = jnp.einsum('bsd,nd->bsn', inputs, weights_in)

            def step(prev_idx, _):
                sel = jnp.clip(prev_idx, 0, max_index)
                logits = jnp.take_along_axis(all_logits, sel[..., None], axis=-1)[..., 0]
                new_idx = jnp.clip(2 * sel + 1 + (logits > 0).astype(sel.dtype), 0, max_index)
                return (new_idx, (logits, new_idx))
            idx0 = jnp.zeros((B, S), dtype=jnp.int32)
            _, (logits_seq, idx_seq) = jax.lax.scan(step, idx0, None, length=depth - 1)
            logits = jnp.concatenate([jnp.zeros((1, B, S), all_logits.dtype), logits_seq], axis=0)
            node_idx = jnp.concatenate([idx0[None], idx_seq], axis=0)
            act = jax.nn.gelu(logits, approximate=False)
            onehot = jax.nn.one_hot(node_idx, n_nodes, dtype=act.dtype)
            coeff = jnp.einsum('dbs,dbsn->bsn', act, onehot)
            return jnp.einsum('bsn,nd->bsd', coeff, weights_out)
        return _fff_forward(inputs, weights_in, weights_out)

    def _L1_gnn_ref(x, edge_index, W, b):
        import jax, jax.numpy as jnp
        import numpy as np
        N_NODES = 1250
        n = x.shape[0]
        loops = jnp.arange(n, dtype=edge_index.dtype)
        row = jnp.concatenate([edge_index[0], loops])
        col = jnp.concatenate([edge_index[1], loops])
        ones = jnp.ones(row.shape[0], dtype=x.dtype)
        deg = jax.ops.segment_sum(ones, col, num_segments=n)
        dinv = jnp.where(deg > 0, jax.lax.rsqrt(deg), 0.0)
        norm = dinv[row] * dinv[col]
        h = x @ W
        msg = h[row] * norm[:, None]
        out = jax.ops.segment_sum(msg, col, num_segments=n) + b
        return out

    def _L1_mix_ref(x, Wq, Wk, Wv, Wo, proj):
        import jax, jax.numpy as jnp
        import numpy as np
        DIM = 768
        HEADS = 12
        DH = DIM // HEADS
        M = 256
        EPS = 0.0001

        def softmax_kernel(data, proj, is_query):
            data_normalizer = data.shape[-1] ** (-0.25)
            ratio = proj.shape[0] ** (-0.5)
            data_dash = jnp.einsum('bhsd,md->bhsm', data_normalizer * data, proj)
            diag = 0.5 * data_normalizer ** 2 * jnp.sum(data * data, axis=-1, keepdims=True)
            if is_query:
                stab = jnp.max(data_dash, axis=-1, keepdims=True)
            else:
                stab = jnp.max(data_dash, axis=(-2, -1), keepdims=True)
            stab = jax.lax.stop_gradient(stab)
            return ratio * (jnp.exp(data_dash - diag - stab) + EPS)
        B, S, _ = x.shape

        def split_heads(t):
            return t.reshape(B, S, HEADS, DH).transpose(0, 2, 1, 3)
        q = split_heads(x @ Wq)
        k = split_heads(x @ Wk)
        v = split_heads(x @ Wv)
        qp = softmax_kernel(q, proj, is_query=True)
        kp = softmax_kernel(k, proj, is_query=False)
        k_sum = jnp.sum(kp, axis=2)
        d_inv = 1.0 / jnp.einsum('bhsm,bhm->bhs', qp, k_sum)
        ctx = jnp.einsum('bhsm,bhsd->bhmd', kp, v)
        out = jnp.einsum('bhsm,bhmd,bhs->bhsd', qp, ctx, d_inv)
        out = out.transpose(0, 2, 1, 3).reshape(B, S, DIM)
        return out @ Wo

    def _L1_ffn_ref(x, ln1_w, ln2_w, c_attn_w, c_proj_w, w_g, c_fc, c_proj_e):
        import jax, jax.numpy as jnp
        import numpy as np
        import math
        N_HEAD = 12
        N_EXP = 8
        TOP_K = 2
        EVAL_CAPACITY = 1.0
        MIN_CAPACITY = 4
        EPS = 1e-05

        def layer_norm(x, w):
            mu = jnp.mean(x, axis=-1, keepdims=True)
            var = jnp.var(x, axis=-1, keepdims=True)
            return (x - mu) / jnp.sqrt(var + EPS) * w

        def attention(x, c_attn_w, c_proj_w):
            B, T, C = x.shape
            H, D = (N_HEAD, C // N_HEAD)
            qkv = x @ c_attn_w.T
            q, k, v = jnp.split(qkv, 3, axis=-1)
            q = q.reshape(B, T, H, D).transpose(0, 2, 1, 3)
            k = k.reshape(B, T, H, D).transpose(0, 2, 1, 3)
            v = v.reshape(B, T, H, D).transpose(0, 2, 1, 3)
            scores = jnp.einsum('bhqd,bhkd->bhqk', q, k) * (1.0 / math.sqrt(D))
            causal = jnp.tril(jnp.ones((T, T), dtype=bool))
            scores = jnp.where(causal, scores, -jnp.inf)
            att = jax.nn.softmax(scores, axis=-1)
            y = jnp.einsum('bhqk,bhkd->bhqd', att, v)
            y = y.transpose(0, 2, 1, 3).reshape(B, T, C)
            return y @ c_proj_w.T

        def get_capacity(num_tokens):
            cap = int(math.floor(TOP_K * EVAL_CAPACITY * num_tokens / N_EXP))
            cap += cap % 2
            return max(cap, MIN_CAPACITY)

        def moe(x_flat, w_g, c_fc, c_proj_e):
            n_tok, C = x_flat.shape
            logits = x_flat @ w_g.T
            top_vals, top_idx = jax.lax.top_k(logits, TOP_K)
            rows = jnp.arange(n_tok)[:, None]
            masked = jnp.full_like(logits, -jnp.inf).at[rows, top_idx].set(top_vals)
            probs = jax.nn.softmax(masked, axis=-1)
            cap = get_capacity(n_tok)
            flat_e = top_idx.reshape(-1)
            onehot = jax.nn.one_hot(flat_e, N_EXP, dtype=jnp.int32)
            pos = jnp.cumsum(onehot, axis=0) - onehot
            slot = jnp.take_along_axis(pos, flat_e[:, None], axis=1)[:, 0]
            valid = slot < cap
            tok = jnp.repeat(jnp.arange(n_tok), TOP_K)
            slot_c = jnp.where(valid, slot, cap)
            sec = jnp.zeros((n_tok, N_EXP, cap + 1), dtype=x_flat.dtype)
            sec = sec.at[tok, flat_e, slot_c].set(1.0)[:, :, :cap]
            w_tok = probs[tok, flat_e]
            cb = jnp.zeros((n_tok, N_EXP, cap + 1), dtype=x_flat.dtype)
            cb = cb.at[tok, flat_e, slot_c].set(w_tok)[:, :, :cap]
            dispatched = jnp.einsum('tec,td->ecd', sec, x_flat)
            h = jax.nn.gelu(jnp.einsum('ecd,edh->ech', dispatched, c_fc), approximate=False)
            out = jnp.einsum('ech,ehd->ecd', h, c_proj_e)
            return jnp.einsum('tec,ecd->td', cb, out)
        x = x + attention(layer_norm(x, ln1_w), c_attn_w, c_proj_w)
        B, T, C = x.shape
        x_ln = layer_norm(x, ln2_w)
        moe_out = moe(x_ln.reshape(B * T, C), w_g, c_fc, c_proj_e)
        return x + moe_out.reshape(B, T, C)
    edge_index = jnp.stack([src, dst])
    xn = _layernorm(x, axis=-1)
    x = x + _L0_gnn_ref(xn, edge_index, L0_gnn_W1, L0_gnn_att_src1, L0_gnn_att_dst1, L0_gnn_b1, L0_gnn_W2, L0_gnn_att_src2, L0_gnn_att_dst2, L0_gnn_b2) + _L0_mix_ref(xn[None], L0_mix_qkv_w, L0_mix_proj_w, L0_mix_proj_b)[0]
    x = x + _L0_ffn_ref(_layernorm(x, axis=-1)[None], L0_ffn_weights_in, L0_ffn_weights_out)[0]
    xn = _layernorm(x, axis=-1)
    x = x + _L1_gnn_ref(xn, edge_index, L1_gnn_W, L1_gnn_b) + _L1_mix_ref(xn[None], L1_mix_Wq, L1_mix_Wk, L1_mix_Wv, L1_mix_Wo, L1_mix_proj)[0]
    x = x + _L1_ffn_ref(_layernorm(x, axis=-1)[None], L1_ffn_ln1_w, L1_ffn_ln2_w, L1_ffn_c_attn_w, L1_ffn_c_proj_w, L1_ffn_w_g, L1_ffn_c_fc, L1_ffn_c_proj_e)[0]
    return x

_drawn_inputs = setup_inputs


def setup_inputs(seed=0):
    import zlib

    import numpy as np

    out = dict(_drawn_inputs(seed))
    spreads = {'L0_gnn_b1': (0.0, 0.1),
     'L0_gnn_b2': (0.0, 0.1),
     'L1_gnn_b': (0.0, 0.8),
     'L1_ffn_ln1_w': (1.0, 0.6),
     'L1_ffn_ln2_w': (1.0, 0.6)}
    factors = {'L0_gnn_att_dst2': 8.0,
     'L0_mix_proj_b': 3.271,
     'L1_gnn_W': 8.0,
     'L1_mix_Wq': 8.0,
     'L1_mix_Wk': 8.0,
     'L1_mix_Wv': 8.0,
     'L1_mix_Wo': 8.0,
     'L1_mix_proj': 8.0,
     'L1_ffn_c_attn_w': 8.0,
     'L1_ffn_c_proj_w': 8.0,
     'L1_ffn_w_g': 8.0,
     'L1_ffn_c_fc': 8.0,
     'L1_ffn_c_proj_e': 8.0}
    for name, (base, spread) in spreads.items():
        noise = np.random.default_rng([zlib.crc32(name.encode()), seed]).standard_normal(out[name].shape)
        drawn = base * np.exp(spread * noise) if base else spread * noise
        out[name] = jnp.asarray(drawn.astype(out[name].dtype))
    for name, factor in factors.items():
        out[name] = (out[name] * factor).astype(out[name].dtype)
    return out
```

```python
from contextlib import ExitStack

import numpy as np

import concourse.bass as bass
from concourse import mybir

F32 = mybir.dt.float32
BF16 = mybir.dt.bfloat16
I32 = mybir.dt.int32
I16 = mybir.dt.int16
U16 = mybir.dt.uint16
ALU = mybir.AluOpType
ACT = mybir.ActivationFunctionType
AX = mybir.AxisListType
RMAX = bass.bass_isa.ReduceOp.max

N = 1250
TP = 125
NT = N // TP
D = 768
KC = D // 128
HALF = D // 2
PAIRS = 6
DH = 64
GH = 4
GD = 512
GK = GD // 128
EDGES = 40000
ET = EDGES // TP
EG = 4
NG = ET // EG
NODES = 21
M = 256
E = 8
CAP = 312
CT = 104
HID = 3072
HC = 6
TRASH = E * CAP
SLOTS = TRASH + 2 * N
NEG = -3.0e38
GROUPS = [(0, 4), (4, 4), (8, 2)]
GC = 250
LN_EPS = 1e-5


class Chain:

    def __init__(self, eng, sem):
        self.eng, self.sem, self.n = eng, sem, 0

    def add(self, ins):
        self.n += 1
        ins.then_inc(self.sem, 1)
        return ins

    def wait(self):
        self.eng.wait_ge(self.sem, self.n)

    def __call__(self, ins):
        self.add(ins)
        self.wait()
        return ins

    def restart(self):
        self.wait()
        self.eng.sem_clear(self.sem)
        self.n = 0


class Ring:

    def __init__(self, sem, name, banks, users):
        self.banks, self.users, self.n = banks, users, len(users)
        self.filled = sem(name + "_filled")
        self.emptied = {u: sem(f"{name}_emptied_by_{u}") for u in sorted(set(users))}
        self.per = {u: users.count(u) for u in self.emptied}

    def bank(self, u):
        return self.banks[u % len(self.banks)]

    def open(self, eng, user):
        if user in self.emptied:
            eng.sem_inc(self.emptied[user], self.per[user])

    def acquire(self, pe, i, u):
        p = u - len(self.banks)
        same = p >= 0
        p %= self.n
        user = self.users[p]
        rank = self.users[:p].count(user)
        pe.wait_ge(self.emptied[user], i * self.per[user] + rank + 1 + (self.per[user] if same else 0))

    def await_filled(self, eng, i, u):
        eng.wait_ge(self.filled, i * self.n + u + 1)

    def give(self, ins, u):
        ins.then_inc(self.emptied[self.users[u]], 1)

    def await_emptied(self, eng, i, u):
        user = self.users[u]
        eng.wait_ge(self.emptied[user], i * self.per[user] + self.users[:u].count(user) + 1 + self.per[user])


def tile_cols(t, count=1):
    return slice(t * TP, (t + count) * TP)


class Program:

    def __init__(self, nc, ctx, d):
        self.nc, self.ctx, self.d = nc, ctx, d
        self.last_phase = None
        self.psA = ctx.enter_context(nc.psum_tensor("psA", [128, 3, 512], F32))
        self.psB = ctx.enter_context(nc.psum_tensor("psB", [128, 3, 512], F32))
        self.psC = ctx.enter_context(nc.psum_tensor("psC", [128, 2, 512], F32))
        self.bank = ([self.psA[:, k, :] for k in range(3)] + [self.psB[:, k, :] for k in range(3)]
                     + [self.psC[:, k, :] for k in range(2)])
        sb = self.persistent
        self.ident = sb("ident", [128, 128], F32)
        self.ones = sb("ones", [128, 128], F32)

    def persistent(self, name, shape, dt):
        return self.ctx.enter_context(self.nc.sbuf_tensor(name, shape, dt))

    def dram(self, name, shape, dt):
        return self.nc.dram_tensor(name, shape, dt, kind="Internal").ap()


class Phase:

    def __init__(self, p, name):
        self.p, self.name = p, name

    def __enter__(self):
        self.ctx, self.sem_ctx, self.sems = ExitStack(), ExitStack(), []
        return self

    def __exit__(self, *a):
        self.ctx.__exit__(*a)
        if self.p.last_phase:
            self.p.last_phase.sem_ctx.close()
        self.p.last_phase = self

    def sb(self, name, shape, dt=F32):
        return self.ctx.enter_context(self.p.nc.sbuf_tensor(f"{self.name}_{name}", shape, dt))

    def sem(self, name):
        self.sems.append(self.sem_ctx.enter_context(self.p.nc.semaphore(f"{self.name}_{name}")))
        return self.sems[-1]

    def ring(self, name, banks, users):
        return Ring(self.sem, name, [self.p.bank[b] for b in banks], users)

    def block(self):
        block = self.ctx.enter_context(self.p.nc.Block())
        if self.p.last_phase:
            @block.gpsimd
            def _(pool):
                for s in self.p.last_phase.sems:
                    pool.sem_clear(s)
        return block



def setup_phase(p):
    with Phase(p, "setup") as f:
        made = f.sem("made")
        block = f.block()

        @block.gpsimd
        def _(pool):
            pool.memset(p.ident[:], 0.0).then_inc(made, 1)
            pool.memset(p.ones[:], 1.0).then_inc(made, 1)
            pool.wait_ge(made, 2)
            pool.affine_select(out=p.ident[:], in_=p.ident[:], compare_op=ALU.not_equal, fill=1.0, base=0,
                               pattern=[[-1, 128]], channel_multiplier=1).then_inc(made, 1)
            pool.wait_ge(made, 3)



def adjacency_phase(p):
    with Phase(p, "adj") as f:
        src_i, dst_i = f.sb("src_i", [TP, ET], I32), f.sb("dst_i", [TP, ET], I32)
        src, dst = f.sb("src", [TP, ET]), f.sb("dst", [TP, ET])
        iota = f.sb("iota", [TP, N], I16)
        up, down = f.sb("up", [TP, NG, EG]), f.sb("down", [TP, NG, EG])
        at_least, inside, scratch = (f.sb(s, [TP, ET]) for s in ("at_least", "inside", "scratch"))
        last = f.sb("last", [TP, 2 * NT])
        every = f.sb("every", [TP, 2 * NT])
        first = f.sb("first", [TP, NT])
        turns = f.sb("turns", [TP, NT])
        limits = f.sb("limits", [TP, 2 * NT], I32)
        of_src = f.sb("of_src", [TP, EG, N], BF16)
        of_dst = f.sb("of_dst", [TP, EG, TP], BF16)
        eye = f.sb("eye", [TP, TP], BF16)
        wide_eye = f.sb("wide_eye", [TP, 2 * N], BF16)
        nothing = f.sb("nothing", [TP, 512], BF16)
        rows = f.sb("rows", [TP, 2, N])
        edges_in, consts, ranges, reduced, limits_ready = (
            f.sem(s) for s in ("edges_in", "consts", "ranges", "reduced", "limits_ready"))
        one_hots, used, cleared, rows_ready = (f.sem(s) for s in ("one_hots", "used", "cleared", "rows_ready"))
        dve_step, block_summed, begun = f.sem("dve_step"), f.sem("block_summed"), f.sem("begun")
        turned = f.ring("turned", [6, 7], ["dve"] * 6)
        sums = [p.psA, p.psB]
        parts = [(0, 512), (512, 512), (1024, N - 1024)]
        block = f.block()

        @block.sync
        def _(sp):
            sp.dma_start(src_i[:], p.d["src"]).then_inc(edges_in, 16)
            sp.dma_start(dst_i[:], p.d["dst"]).then_inc(edges_in, 16)
            sp.wait_ge(edges_in, 32)

        @block.gpsimd
        def _(pool):
            pool.iota(iota[:], [[1, N]], base=0, channel_multiplier=0).then_inc(consts, 1)
            pool.iota(up[:], [[1, NG], [0, EG]], base=1, channel_multiplier=0,
                      allow_small_or_imprecise_dtypes=True).then_inc(consts, 1)
            pool.iota(down[:], [[-1, NG], [0, EG]], base=NG, channel_multiplier=0,
                      allow_small_or_imprecise_dtypes=True).then_inc(consts, 1)
            pool.memset(eye[:], 0.0).then_inc(consts, 1)
            pool.memset(wide_eye[:], 0.0).then_inc(consts, 1)
            pool.memset(nothing[:], 0.0).then_inc(consts, 1)
            pool.wait_ge(consts, 6)
            pool.affine_select(out=eye[:], in_=eye[:], compare_op=ALU.not_equal, fill=1.0, base=0,
                               pattern=[[-1, TP]], channel_multiplier=1).then_inc(consts, 1)
            pool.affine_select(out=wide_eye[:], in_=wide_eye[:], compare_op=ALU.not_equal, fill=1.0,
                               base=N - TP, pattern=[[-1, 2 * N]], channel_multiplier=1).then_inc(consts, 1)
            pool.wait_ge(consts, 8)
            pool.wait_ge(ranges, 2 * NT)
            pool.partition_all_reduce(every[:], last[:], TP, RMAX).then_inc(reduced, 1)

        @block.vector
        def _(dve):
            step = Chain(dve, dve_step)
            turned.open(dve, "dve")
            dve.wait_ge(consts, 8)
            dve.wait_ge(edges_in, 32)
            step.add(dve.tensor_copy(src[:], src_i[:]))
            step(dve.tensor_copy(dst[:], dst_i[:]))
            flat = "p a b -> p (a b)"
            for c in range(NT):
                step(dve.tensor_scalar(at_least[:], dst[:], float(c * TP), None, ALU.is_ge))
                step(dve.scalar_tensor_tensor(inside[:], dst[:], float(c * TP + TP), at_least[:],
                                              ALU.is_lt, ALU.mult))
                for n, of in ((0, up), (NT, down)):
                    dve.tensor_tensor_reduce(out=scratch[:], in0=inside[:], in1=of[:].rearrange(flat), scale=1.0,
                                             scalar=0.0, op0=ALU.mult, op1=ALU.max,
                                             accum_out=last[:, n + c:n + c + 1]).then_inc(ranges, 1)
                    dve.wait_ge(ranges, 2 * c + (2 if n else 1))
            dve.wait_ge(reduced, 1)
            step(dve.tensor_scalar(first[:], every[:, NT:2 * NT], -1.0, float(NG), ALU.mult, ALU.add))
            step(dve.tensor_scalar(first[:], first[:], float(NG - 1), None, ALU.min))
            step(dve.tensor_tensor(turns[:], every[:, 0:NT], first[:], ALU.subtract))
            step(dve.tensor_scalar(limits[:, NT:2 * NT], turns[:], 1.0, None, ALU.max))
            dve.tensor_copy(limits[:, 0:NT], first[:]).then_inc(limits_ready, 1)
            dve.wait_ge(limits_ready, 1)
            with dve.Fori(0, NT // 2) as i:
                for b in range(2):
                    c = i * 2 + b
                    start = dve.value_load(limits[0:1, bass.ds(c, 1)], min_val=0, max_val=NG - 1)
                    count = dve.value_load(limits[0:1, bass.ds(c + NT, 1)], min_val=1, max_val=NG)
                    dve.wait_ge(block_summed, c)
                    dve.sem_inc(begun, 1)
                    dve.sem_clear(one_hots)
                    dve.sem_clear(used)
                    dve.sem_inc(used, EG)
                    dve.sem_inc(cleared, 1)
                    with dve.Fori(0, count) as j:
                        group = p.nc.s_assert_within(
                            start + j, 0, NG - 1,
                            skip_runtime_bounds_check_because="count is the last group less start, plus one")
                        for k in range(EG):
                            dve.wait_ge(used, j * EG + k + 1)
                            e = group * EG + k
                            dve.tensor_scalar(of_src[:, k, :], iota[:], src[:, bass.ds(e, 1)], None, ALU.is_equal)
                            dve.tensor_scalar(of_dst[:, k, :], iota[:, bass.ds(c * TP, TP)], dst[:, bass.ds(e, 1)],
                                              None, ALU.is_equal).then_inc(one_hots, 1)
                    for g, (t0, n) in enumerate(GROUPS):
                        turned.await_filled(dve, i, 3 * b + g)
                        turned.give(dve.tensor_copy(
                            p.AT[:, t0:t0 + n, bass.ds(c * TP, TP)],
                            turned.bank(3 * b + g)[0:TP, 0:n * TP].rearrange("p (a b) -> p a b", a=n)), 3 * b + g)
            turned.await_emptied(dve, NT // 2 - 1, 5)
            dve.wait_ge(begun, NT)

        @block.tensor
        def _(pe):
            pe.wait_ge(consts, 8)
            pe.wait_ge(limits_ready, 1)
            with pe.Fori(0, NT // 2) as i:
                for b in range(2):
                    c = i * 2 + b
                    out = sums[b][0:TP, :, :].rearrange("p a b -> p (a b)")
                    count = pe.value_load(limits[0:1, bass.ds(c + NT, 1)], min_val=1, max_val=NG)
                    pe.wait_ge(cleared, c + 1)
                    pe.wait_ge(rows_ready, c + 1)
                    for a, w in parts:
                        pe.matmul(out[:, a:a + w], eye[:], nothing[:, 0:w], start=True, stop=False)
                    with pe.Fori(0, count) as j:
                        for k in range(EG):
                            pe.wait_ge(one_hots, j * EG + k + 1)
                            for a, w in parts:
                                mm = pe.matmul(out[:, a:a + w], of_dst[:, k, :], of_src[:, k, a:a + w],
                                               start=False, stop=False)
                            mm.then_inc(used, 1)
                    for a, w in parts:
                        mm = pe.matmul(out[:, a:a + w], eye[:], wide_eye[:, bass.ds(N - TP - c * TP + a, w)],
                                       start=False, stop=True)
                    mm.then_inc(block_summed, 1)
                    pe.wait_ge(rows_ready, c + 3)
                    for g, (t0, n) in enumerate(GROUPS):
                        turned.acquire(pe, i, 3 * b + g)
                        for q in range(n):
                            mm = pe.transpose(turned.bank(3 * b + g)[0:TP, tile_cols(q)],
                                              rows[:, b, tile_cols(t0 + q)], p.ident[0:TP, 0:TP])
                        mm.then_inc(turned.filled, 1)

        @block.scalar
        def _(act):
            act.sem_inc(rows_ready, 2)
            with act.Fori(0, NT // 2) as i:
                for b in range(2):
                    act.wait_ge(block_summed, i * 2 + b + 1)
                    act.copy(rows[:, b, :],
                             sums[b][0:TP, :, :].rearrange("p a b -> p (a b)")[:, 0:N]).then_inc(rows_ready, 1)



def layer_norm_phase(p, name, x_in, xn, w_name=None, plain=None, transposed=True):
    with Phase(p, name) as f:
        stats = f.sb("stats", [TP, NT, 2, 6])
        mv = f.sb("mean_var", [TP, NT, 2])
        var = f.sb("var_eps", [TP, NT])
        std = f.sb("std", [TP, NT])
        rstd = f.sb("rstd", [TP, NT])
        w = f.sb("w", [TP, D]) if w_name else None
        var_ready, std_ready, xn_ready = f.sem("var_ready"), f.sem("std_ready"), f.sem("xn_ready")
        dve_step, w_in = f.sem("dve_step"), f.sem("w_in")
        units = [(g, k) for g in range(len(GROUPS)) for k in range(KC)]
        ring = f.ring("transposed", range(8), (["dve", "act"] * len(units))[:len(units)])
        block = f.block()

        def empty(eng, copy, user):
            for u, (g, k) in enumerate(units):
                if ring.users[u] == user:
                    t, n = GROUPS[g]
                    ring.await_filled(eng, 0, u)
                    ring.give(copy(p.xT[:, k, tile_cols(t, n)], ring.bank(u)[:, 0:n * TP]), u)
            if ring.per[user]:
                eng.wait_ge(ring.emptied[user], 2 * ring.per[user])

        if w_name:
            @block.sync
            def _(sp):
                sp.dma_start(w[:], p.d[w_name].partition_broadcast(TP)).then_inc(w_in, 16)
                sp.wait_ge(w_in, 16)

        @block.vector
        def _(dve):
            step = Chain(dve, dve_step)
            if transposed:
                ring.open(dve, "dve")
            for t in range(NT):
                for h in range(2):
                    step.add(dve.bn_stats(stats[:, t, h, :], x_in[:, t, h * HALF:(h + 1) * HALF]))
            step.wait()
            for t in range(NT):
                step.add(dve.bn_aggr(mv[:, t, :], stats[:, t, :, :].rearrange("p a b -> p (a b)")))
            step.wait()
            dve.tensor_scalar(var[:], mv[:, :, 1], LN_EPS, None, ALU.add).then_inc(var_ready, 1)
            dve.wait_ge(std_ready, 1)
            step(dve.reciprocal(rstd[:], std[:]))
            if w_name:
                dve.wait_ge(w_in, 16)
            for t in range(NT):
                y = plain[:, t % 2, :] if w_name else xn[:, t, :]
                if w_name and t >= 2:
                    dve.wait_ge(xn_ready, t - 1)
                ins = dve.tensor_scalar(y, x_in[:, t, :], mv[:, t, 0:1], rstd[:, t:t + 1],
                                        ALU.subtract, ALU.mult)
                if w_name:
                    step(ins)
                    ins = dve.tensor_tensor(xn[:, t, :], y, w[:], ALU.mult)
                ins.then_inc(xn_ready, 1)
            dve.wait_ge(xn_ready, NT)
            if transposed:
                empty(dve, dve.tensor_copy, "dve")

        @block.scalar
        def _(act):
            if transposed:
                ring.open(act, "act")
            act.wait_ge(var_ready, 1)
            act.activation(std[:], var[:], ACT.Sqrt).then_inc(std_ready, 1)
            if transposed:
                empty(act, act.copy, "act")

        if transposed:
            @block.tensor
            def _(pe):
                for u, (g, k) in enumerate(units):
                    t0, n = GROUPS[g]
                    pe.wait_ge(xn_ready, t0 + n)
                    ring.acquire(pe, 0, u)
                    for j in range(n):
                        mm = pe.transpose(ring.bank(u)[:, tile_cols(j)], xn[:, t0 + j, k * 128:(k + 1) * 128],
                                          p.ident[0:TP, 0:TP])
                    mm.then_inc(ring.filled, 1)



def projection_phase(p, name, yT, w_name, res, bias=None, also=None):
    with Phase(p, name) as f:
        w = f.sb("w", [128, KC, D])
        b = f.sb("b", [TP, D]) if bias else None
        w_in, b_in, biased, added, summed = (f.sem(s) for s in ("w_in", "b_in", "biased", "added", "summed"))
        units = [(t, h) for t in range(NT) for h in range(2)]
        ring = f.ring("product", range(8), ["dve"] * len(units))
        block = f.block()

        @block.sync
        def _(sp):
            sp.dma_start(w[:], p.d[w_name].rearrange("p (k n) -> p k n", k=KC)).then_inc(w_in, 16)
            if bias:
                sp.dma_start(b[:], p.d[bias].partition_broadcast(TP)).then_inc(b_in, 16)
                sp.wait_ge(b_in, 16)

        @block.gpsimd
        def _(pool):
            if bias:
                pool.wait_ge(b_in, 16)
                for t in range(NT):
                    pool.tensor_tensor(res[:, t, :], res[:, t, :], b[:], ALU.add).then_inc(biased, 1)
                pool.wait_ge(biased, NT)
            if also is not None:
                for t in range(NT):
                    pool.wait_ge(ring.emptied["dve"], 2 * NT + 2 * t + 2)
                    pool.tensor_tensor(also[:, t, :], also[:, t, :], res[:, t, :], ALU.add).then_inc(summed, 1)
                pool.wait_ge(summed, NT)

        @block.tensor
        def _(pe):
            pe.wait_ge(w_in, 16)
            for u, (t, h) in enumerate(units):
                ring.acquire(pe, 0, u)
                for k in range(KC):
                    mm = pe.matmul(ring.bank(u)[0:TP, 0:HALF], yT[:, k, tile_cols(t)],
                                   w[:, k, h * HALF:(h + 1) * HALF], start=(k == 0), stop=(k == KC - 1))
                mm.then_inc(ring.filled, 1)

        @block.vector
        def _(dve):
            ring.open(dve, "dve")
            for u, (t, h) in enumerate(units):
                if bias:
                    dve.wait_ge(biased, t + 1)
                ring.await_filled(dve, 0, u)
                r = res[:, t, h * HALF:(h + 1) * HALF]
                ring.give(dve.tensor_tensor(r, ring.bank(u)[0:TP, 0:HALF], r, ALU.add), u)
            ring.await_emptied(dve, 0, len(units) - 1)



def linear_attention_phase(p, yT):
    with Phase(p, "lin") as f:
        w = f.sb("w", [128, KC, 384])
        q_exp, q_relu = f.sb("q_exp", [128, N]), f.sb("q_relu", [128, N])
        qT = f.sb("qT", [128, N])
        k_exp, k_relu = f.sb("k_exp", [TP, NT, 128]), f.sb("k_relu", [TP, NT, 128])
        k = f.sb("k", [TP, NT, 128])
        v1 = f.sb("v1", [TP, NT, 132])
        same_head = f.sb("same_head", [128, 132])
        state = f.sb("state", [128, 132])
        den, rden = f.sb("den", [TP, NT, 2]), f.sb("rden", [TP, NT, 2])
        y = f.sb("y", [TP, NT, 128])
        w_in, q_ready, k_ready, state_ready = (f.sem(s) for s in ("w_in", "q_ready", "k_ready", "state_ready"))
        dve_step, made = f.sem("dve_step"), f.sem("made")
        wide = f.ring("wide", [0, 1, 2], ["act"] * 6)
        kv = f.ring("kv", [3, 4], ["act"] * NT)
        acc = f.ring("acc", [5], ["dve"])
        out = f.ring("out", [6, 7], ["dve"] * NT)
        block = f.block()

        @block.sync
        def _(sp):
            with sp.Fori(0, PAIRS) as i:
                sp.wait_ge(kv.filled, i * NT)
                sp.dma_start(w[:], p.d["qkv0"][bass.ds(i, 1), :, :]).then_inc(w_in, 16)

        @block.gpsimd
        def _(pool):
            pool.memset(same_head[:], 0.0).then_inc(made, 1)
            pool.memset(v1[:], 1.0).then_inc(made, 1)
            pool.wait_ge(made, 2)
            for h in range(2):
                rows = slice(h * DH, (h + 1) * DH)
                pool.memset(same_head[rows, rows], 1.0).then_inc(made, 1)
                pool.memset(same_head[rows, 128 + h:129 + h], 1.0).then_inc(made, 1)
            pool.wait_ge(made, 6)

        @block.tensor
        def _(pe):
            pe.wait_ge(made, 6)
            with pe.Fori(0, PAIRS) as i:
                pe.wait_ge(w_in, i * 16 + 16)
                for g, (t0, n) in enumerate(GROUPS):
                    wide.acquire(pe, i, g)
                    for c in range(KC):
                        mm = pe.matmul(wide.bank(g)[:, 0:n * TP], w[:, c, 0:128], p.xT[:, c, tile_cols(t0, n)],
                                       start=(c == 0), stop=(c == KC - 1))
                    mm.then_inc(wide.filled, 1)
                for t in range(NT):
                    kv.acquire(pe, i, t)
                    for c in range(KC):
                        mm = pe.matmul(kv.bank(t)[0:TP, 0:256], p.xT[:, c, tile_cols(t)], w[:, c, 128:384],
                                       start=(c == 0), stop=(c == KC - 1))
                    mm.then_inc(kv.filled, 1)
                acc.acquire(pe, i, 0)
                for t in range(NT):
                    pe.wait_ge(k_ready, i * NT + t + 1)
                    kv.await_emptied(pe, i, t)
                    mm = pe.matmul(acc.bank(0)[:, 0:130], k[:, t, :], v1[:, t, 0:130],
                                   start=(t == 0), stop=(t == NT - 1))
                mm.then_inc(acc.filled, 1)
                pe.wait_ge(q_ready, i * 3 + 3)
                acc.await_emptied(pe, i, 0)
                for t in range(NT):
                    out.acquire(pe, i, t)
                    pe.matmul(out.bank(t)[0:TP, 0:130], qT[:, tile_cols(t)], state[:, 0:130],
                              start=True, stop=True).then_inc(out.filled, 1)
                for g, (t0, n) in enumerate(GROUPS):
                    out.await_emptied(pe, i, t0 + n - 1)
                    wide.acquire(pe, i, 3 + g)
                    for j in range(n):
                        mm = pe.transpose(wide.bank(g)[:, tile_cols(j)], y[:, t0 + j, :], p.ident[0:TP, 0:TP])
                    mm.then_inc(wide.filled, 1)

        @block.scalar
        def _(act):
            wide.open(act, "act")
            kv.open(act, "act")
            act.wait_ge(made, 6)
            with act.Fori(0, PAIRS) as i:
                act.wait_ge(q_ready, i * 3)
                act.wait_ge(k_ready, i * NT)
                for g, (t0, n) in enumerate(GROUPS):
                    wide.await_filled(act, i, g)
                    cols = tile_cols(t0, n)
                    act.activation(q_exp[:, cols], wide.bank(g)[:, 0:n * TP], ACT.Exp)
                    wide.give(act.activation(q_relu[:, cols], wide.bank(g)[:, 0:n * TP], ACT.Relu), g)
                for t in range(NT):
                    kv.await_filled(act, i, t)
                    act.activation(k_exp[:, t, :], kv.bank(t)[0:TP, 0:128], ACT.Exp)
                    act.activation(k_relu[:, t, :], kv.bank(t)[0:TP, 0:128], ACT.Relu)
                    kv.give(act.copy(v1[:, t, 0:128], kv.bank(t)[0:TP, 128:256]), t)
                for g, (t0, n) in enumerate(GROUPS):
                    wide.await_filled(act, i, 3 + g)
                    wide.give(act.copy(yT[:, bass.ds(i, 1), tile_cols(t0, n)], wide.bank(g)[:, 0:n * TP]), 3 + g)
            wide.await_emptied(act, PAIRS - 1, 5)

        @block.vector
        def _(dve):
            step = Chain(dve, dve_step)
            acc.open(dve, "dve")
            out.open(dve, "dve")
            dve.wait_ge(made, 6)
            with dve.Fori(0, PAIRS) as i:
                step.restart()
                for g, (t0, n) in enumerate(GROUPS):
                    wide.await_emptied(dve, i, g)
                    cols = tile_cols(t0, n)
                    dve.scalar_tensor_tensor(qT[:, cols], q_exp[:, cols], 1.0, q_relu[:, cols],
                                             ALU.min, ALU.add).then_inc(q_ready, 1)
                for t in range(NT):
                    kv.await_emptied(dve, i, t)
                    dve.scalar_tensor_tensor(k[:, t, :], k_exp[:, t, :], 1.0, k_relu[:, t, :],
                                             ALU.min, ALU.add).then_inc(k_ready, 1)
                acc.await_filled(dve, i, 0)
                dve.tensor_tensor(state[:, 0:128], acc.bank(0)[:, 0:128], same_head[:, 0:128], ALU.mult)
                acc.give(dve.tensor_tensor(state[:, 128:130], acc.bank(0)[:, 128:129].to_broadcast([128, 2]),
                                           same_head[:, 128:130], ALU.mult), 0)
                for t in range(NT):
                    out.await_filled(dve, i, t)
                    step(dve.tensor_scalar(den[:, t, :], out.bank(t)[0:TP, 128:130], 1e-6, None, ALU.add))
                    step(dve.reciprocal(rden[:, t, :], den[:, t, :]))
                    out.give(dve.tensor_tensor(
                        y[:, t, :].rearrange("p (h e) -> p h e", h=2),
                        out.bank(t)[0:TP, 0:128].rearrange("p (h e) -> p h e", h=2),
                        rden[:, t, :].unsqueeze(2).to_broadcast([TP, 2, DH]), ALU.mult), t)
            dve.wait_ge(dve_step, step.n)



class GatCore:

    STEPS = N // GC

    def __init__(self, f, p, h, width, before):
        self.f, self.p, self.h, self.width = f, p, h, width
        sb = f.sb
        self.a_src, self.a_dst = sb("a_src", [TP, width]), sb("a_dst", [TP, width])
        self.scratch = sb("scratch", [TP, width])
        self.al_s, self.al_d, self.al_s2 = sb("al_s", [TP, NT]), sb("al_d", [TP, NT]), sb("al_s2", [TP, NT])
        self.no_edge = sb("no_edge", [TP, 2, N], BF16)
        self.acc = sb("acc", [TP, N])
        self.top, self.z, self.mx = sb("top", [TP, NT]), sb("z", [TP, NT]), sb("mx", [TP, NT])
        self.r = sb("r", [TP, 2, NT])
        self.diag = sb("diag", [TP, 4, TP])
        self.rows = sb("rows", [TP, 2, N])
        self.e1 = sb("e1", [TP, 2, NT, GC])
        self.e2 = sb("e2", [TP, 2, NT // 2, GC])
        self.sums = sb("sums", [TP, 2])
        self.rden = sb("rden", [TP, 2])
        self.vectors_in = f.sem("vectors_in")
        self.diag_used = f.sem("diag_used")
        self.al_ready, self.mask_step, self.acc_ready = f.sem("al_ready"), f.sem("mask_step"), f.sem("acc_ready")
        self.diag_ready, self.exps_ready, self.p_ready = f.sem("diag_ready"), f.sem("exps_ready"), f.sem("p_ready")
        self.al_s2_ready = f.sem("al_s2_ready")
        self.misc = f.ring("misc", [0, 1], before + ["dve"] * 4 + ["act"] * 6)
        self.base = len(before)
        self.den = f.ring("den", [2], ["dve"] * self.STEPS)
        self.top_groups = [(0, 3), (3, 3), (6, 2), (8, 2)]


    def turn_maxima(self, pe, i):
        pe.wait_ge(self.acc_ready, i + 1)
        for g, (t0, n) in enumerate(self.top_groups):
            u = self.base + g
            self.misc.acquire(pe, i, u)
            for j in range(n):
                mm = pe.transpose(self.misc.bank(u)[0:TP, tile_cols(j)], self.acc[:, tile_cols(t0 + j)],
                                  self.p.ident[0:TP, 0:TP])
            mm.then_inc(self.misc.filled, 1)

    def spread_rows(self, pe, i):
        m = 0
        for r in range(2):
            for g, (t0, n) in enumerate(GROUPS):
                u = self.base + 4 + 3 * r + g
                self.misc.acquire(pe, i, u)
                for j in range(n):
                    pe.wait_ge(self.diag_ready, i * 2 * NT + m + 1)
                    mm = pe.matmul(self.misc.bank(u)[0:TP, tile_cols(j)], self.p.ones[0:TP, 0:TP],
                                   self.diag[:, m % 4, :], start=True, stop=True)
                    m += 1
                    if j < n - 1:
                        mm.then_inc(self.diag_used, 1)
                mm.then_inc(self.misc.filled, 1)

    def denominators(self, pe, i, ch):
        pe.wait_ge(self.p_ready, i * 2 * self.STEPS + 2 * ch + 2)
        self.den.acquire(pe, i, ch)
        for td in range(2):
            for j in range(NT):
                mm = pe.matmul(self.den.bank(0)[0:TP, td:td + 1], self.e1[:, ch % 2, j, tile_cols(td)],
                               self.p.ones[0:TP, 0:1], start=(j == 0), stop=(j == NT - 1))
        mm.then_inc(self.den.filled, 1)


    def maxima(self, dve, step, i, await_h):
        dve.wait_ge(self.vectors_in, i * 32 + 32)
        for t in range(NT):
            if await_h:
                await_h(t)
            for a, al in ((self.a_src, self.al_s), (self.a_dst, self.al_d)):
                step(dve.tensor_tensor_reduce(out=self.scratch[:], in0=self.h[:, t, :], in1=a[:], scale=1.0,
                                              scalar=0.0, op0=ALU.mult, op1=ALU.add,
                                              accum_out=al[:, t:t + 1]))
        dve.tensor_scalar(self.al_s2[:], self.al_s[:], 0.2, None, ALU.mult).then_inc(self.al_s2_ready, 1)
        for j in range(NT):
            step(dve.tensor_scalar(self.no_edge[:, j % 2, :], self.p.AT[:, j, :], 0.0, NEG,
                                   ALU.is_equal, ALU.mult))
            if j == 0:
                ins = dve.tensor_scalar(self.acc[:], self.no_edge[:, 0, :], self.al_s[:, 0:1], None, ALU.add)
            else:
                ins = dve.scalar_tensor_tensor(self.acc[:], self.no_edge[:, j % 2, :], self.al_s[:, j:j + 1],
                                               self.acc[:], ALU.add, ALU.max)
            if j < NT - 1:
                step.add(ins)
            else:
                ins.then_inc(self.acc_ready, 1)

    def columns(self, dve, step, i):
        for g, (t0, n) in enumerate(self.top_groups):
            u = self.base + g
            self.misc.await_filled(dve, i, u)
            self.misc.give(dve.tensor_reduce(self.top[:, t0:t0 + n],
                                             self.misc.bank(u)[0:TP, 0:n * TP].rearrange("p (a b) -> p a b", a=n),
                                             AX.X, ALU.max), u)
        self.misc.await_emptied(dve, i, self.base + 3)
        step(dve.tensor_tensor(self.z[:], self.top[:], self.al_d[:], ALU.add))
        step(dve.scalar_tensor_tensor(self.mx[:], self.z[:], 0.2, self.z[:], ALU.mult, ALU.max))
        step.add(dve.tensor_tensor(self.r[:, 0, :], self.al_d[:], self.mx[:], ALU.subtract))
        step(dve.scalar_tensor_tensor(self.r[:, 1, :], self.al_d[:], 0.2, self.mx[:], ALU.mult, ALU.subtract))
        for m in range(2 * NT):
            r, t = divmod(m, NT)
            self.await_diag_used(dve, i, m)
            dve.tensor_scalar(self.diag[:, m % 4, :], self.p.ident[0:TP, 0:TP], self.r[:, r, t:t + 1], None,
                              ALU.mult).then_inc(self.diag_ready, 1)

    def await_diag_used(self, dve, i, m):
        if m < 4:
            return
        r, t = divmod(m - 4, NT)
        g = next(g for g, (t0, n) in enumerate(GROUPS) if t0 <= t < t0 + n)
        t0, n = GROUPS[g]
        if t == t0 + n - 1:
            self.misc.await_filled(dve, i, self.base + 4 + 3 * r + g)
        else:
            dve.wait_ge(self.diag_used, i * 14 + r * 7 + t - g + 1)

    def weights(self, dve, step, i, ch, half):
        n = 2 * ch + half
        dve.wait_ge(self.exps_ready, i * 2 * self.STEPS + n + 1)
        js = slice(half * 5, half * 5 + 5)
        e1 = self.e1[:, ch % 2, js, :]
        step(dve.tensor_tensor(e1, e1, self.e2[:, half, :, :], ALU.max))
        dve.scalar_tensor_tensor(e1, e1, 1.0, self.p.AT[:, js, ch * GC:(ch + 1) * GC],
                                 ALU.min, ALU.mult).then_inc(self.p_ready, 1)

    def reciprocals(self, dve, step, i, ch):
        self.den.await_filled(dve, i, ch)
        self.den.give(dve.tensor_scalar(self.sums[:], self.den.bank(0)[0:TP, 0:2], 1e-16, None, ALU.add), ch)
        self.den.await_emptied(dve, i, ch)
        step(dve.reciprocal(self.rden[:], self.sums[:]))


    def empty_rows(self, act, i):
        for r in range(2):
            for g, (t0, n) in enumerate(GROUPS):
                u = self.base + 4 + 3 * r + g
                self.misc.await_filled(act, i, u)
                self.misc.give(act.copy(self.rows[:, r, tile_cols(t0, n)], self.misc.bank(u)[0:TP, 0:n * TP]), u)
        self.misc.await_emptied(act, i, self.base + 9)
        act.wait_ge(self.al_s2_ready, i + 1)

    def exponentials(self, act, i, ch, half, agg_count):
        n = 2 * ch + half
        agg_count(act, ch)
        act.wait_ge(self.p_ready, i * 2 * self.STEPS + max(n - 1, 0))
        for k in range(5):
            j = half * 5 + k
            cols = slice(ch * GC, (ch + 1) * GC)
            act.activation(self.e1[:, ch % 2, j, :], self.rows[:, 0, cols], ACT.Exp, bias=self.al_s[:, j:j + 1])
            ins = act.activation(self.e2[:, half, k, :], self.rows[:, 1, cols], ACT.Exp,
                                 bias=self.al_s2[:, j:j + 1])
        ins.then_inc(self.exps_ready, 1)


def gat1_phase(p, h2):
    with Phase(p, "gat1") as f:
        w1, w2 = f.sb("w1", [128, KC, GD]), f.sb("w2", [128, GK, D])
        bias = f.sb("bias", [TP, GD])
        h = f.sb("h", [TP, NT, GD])
        y, ey, ry, z = f.sb("y", [TP, GD]), f.sb("ey", [TP, GD]), f.sb("ry", [TP, GD]), f.sb("elu", [TP, GD])
        zT = f.sb("eluT", [128, 2, GK, TP])
        core = GatCore(f, p, h, GD, ["act"] * NT)
        w1_in, w2_in, y_ready, ey_ready, z_ready = (
            f.sem(s) for s in ("w1_in", "w2_in", "y_ready", "ey_ready", "z_ready"))
        dve_step, bias_in, zeroed = f.sem("dve_step"), f.sem("bias_in"), f.sem("zeroed")
        agg = f.ring("agg", [3, 4], ["dve"] * NT)
        turned = f.ring("turned", [5], ["act"] * NT)
        prod = f.ring("prod", [6, 7], ["dve"] * (2 * NT))
        block = f.block()

        @block.sync
        def _(sp):
            with sp.Fori(0, GH) as i:
                sp.wait_ge(core.misc.filled, i * core.misc.n)
                sp.dma_start(w1[:], p.d["W1"][bass.ds(i, 1), :, :]).then_inc(w1_in, 16)
                sp.wait_ge(core.acc_ready, i)
                sp.dma_start(core.a_src[:], p.d["att_src1"][bass.ds(i, 1), :].partition_broadcast(TP)
                             ).then_inc(core.vectors_in, 16)
                sp.dma_start(core.a_dst[:], p.d["att_dst1"][bass.ds(i, 1), :].partition_broadcast(TP)
                             ).then_inc(core.vectors_in, 16)
                sp.wait_ge(y_ready, i * NT)
                sp.dma_start(bias[:], p.d["b1"][bass.ds(i, 1), :].partition_broadcast(TP)).then_inc(bias_in, 16)
                sp.wait_ge(prod.filled, i * 2 * NT)
                sp.dma_start(w2[:], p.d["W2"][bass.ds(i, 1), :, :]).then_inc(w2_in, 16)

        @block.gpsimd
        def _(pool):
            pool.memset(h2[:], 0.0).then_inc(zeroed, 1)
            pool.wait_ge(zeroed, 1)

        @block.tensor
        def _(pe):
            def turn(i, t):
                pe.wait_ge(z_ready, i * NT + t + 1)
                turned.acquire(pe, i, t)
                for k in range(GK):
                    mm = pe.transpose(turned.bank(0)[:, tile_cols(k)], z[:, k * 128:(k + 1) * 128],
                                      p.ident[0:TP, 0:TP])
                mm.then_inc(turned.filled, 1)

            def times_w2(i, t):
                turned.await_emptied(pe, i, t)
                for half in range(2):
                    u = 2 * t + half
                    prod.acquire(pe, i, u)
                    for k in range(GK):
                        mm = pe.matmul(prod.bank(u)[0:TP, 0:HALF], zT[:, t % 2, k, :],
                                       w2[:, k, half * HALF:(half + 1) * HALF], start=(k == 0), stop=(k == GK - 1))
                    mm.then_inc(prod.filled, 1)

            with pe.Fori(0, GH) as i:
                pe.wait_ge(w1_in, i * 16 + 16)
                for t in range(NT):
                    core.misc.acquire(pe, i, t)
                    for k in range(KC):
                        mm = pe.matmul(core.misc.bank(t)[0:TP, :], p.xT[:, k, tile_cols(t)], w1[:, k, :],
                                       start=(k == 0), stop=(k == KC - 1))
                    mm.then_inc(core.misc.filled, 1)
                core.turn_maxima(pe, i)
                core.spread_rows(pe, i)
                pe.wait_ge(w2_in, i * 16 + 16)
                for t in range(NT):
                    if t % 2 == 0:
                        core.denominators(pe, i, t // 2)
                    agg.acquire(pe, i, t)
                    for j in range(NT):
                        mm = pe.matmul(agg.bank(t)[0:TP, :], core.e1[:, (t // 2) % 2, j, tile_cols(t % 2)],
                                       h[:, j, :], start=(j == 0), stop=(j == NT - 1))
                    mm.then_inc(agg.filled, 1)
                    if t >= 1:
                        turn(i, t - 1)
                    if t >= 2:
                        times_w2(i, t - 2)
                turn(i, NT - 1)
                times_w2(i, NT - 2)
                times_w2(i, NT - 1)

        @block.scalar
        def _(act):
            core.misc.open(act, "act")
            turned.open(act, "act")
            used = lambda eng, i, ch: eng.wait_ge(agg.filled, i * NT + (2 * (ch - 1) if ch >= 2 else 0))
            with act.Fori(0, GH) as i:
                for t in range(NT):
                    core.misc.await_filled(act, i, t)
                    if t == 0:
                        act.wait_ge(agg.filled, i * NT)
                    core.misc.give(act.copy(h[:, t, :], core.misc.bank(t)[0:TP, :]), t)
                core.empty_rows(act, i)
                for half in range(2):
                    core.exponentials(act, i, 0, half, lambda eng, ch: used(eng, i, ch))
                for t in range(NT):
                    ch = t // 2 + 1
                    if ch < core.STEPS:
                        core.exponentials(act, i, ch, t % 2, lambda eng, ch: used(eng, i, ch))
                    act.wait_ge(y_ready, i * NT + t + 1)
                    act.activation(ey[:], y[:], ACT.Exp).then_inc(ey_ready, 1)
                    if t >= 1:
                        turned.await_filled(act, i, t - 1)
                        turned.give(act.copy(zT[:, (t - 1) % 2, :, :], turned.bank(0)[:, 0:GK * TP].rearrange(
                            "p (a b) -> p a b", a=GK)), t - 1)
                turned.await_filled(act, i, NT - 1)
                turned.give(act.copy(zT[:, 1, :, :], turned.bank(0)[:, 0:GK * TP].rearrange(
                    "p (a b) -> p a b", a=GK)), NT - 1)

        @block.vector
        def _(dve):
            step = Chain(dve, dve_step)
            core.misc.open(dve, "dve")
            core.den.open(dve, "dve")
            agg.open(dve, "dve")
            prod.open(dve, "dve")
            dve.wait_ge(zeroed, 1)

            def add_product(i, t):
                for half in range(2):
                    u = 2 * t + half
                    prod.await_filled(dve, i, u)
                    r = h2[:, t, half * HALF:(half + 1) * HALF]
                    prod.give(dve.tensor_tensor(r, prod.bank(u)[0:TP, 0:HALF], r, ALU.add), u)

            with dve.Fori(0, GH) as i:
                step.restart()
                core.maxima(dve, step, i, lambda t: core.misc.await_emptied(dve, i, t))
                core.columns(dve, step, i)
                dve.wait_ge(bias_in, i * 16 + 16)
                for half in range(2):
                    core.weights(dve, step, i, 0, half)
                for t in range(NT):
                    ch = t // 2 + 1
                    if ch < core.STEPS:
                        core.weights(dve, step, i, ch, t % 2)
                    if t % 2 == 0:
                        core.reciprocals(dve, step, i, t // 2)
                    agg.await_filled(dve, i, t)
                    agg.give(dve.scalar_tensor_tensor(y[:], agg.bank(t)[0:TP, :], core.rden[:, t % 2:t % 2 + 1],
                                                      bias[:], ALU.mult, ALU.add), t)
                    agg.await_emptied(dve, i, t)
                    dve.tensor_scalar(ry[:], y[:], 0.0, -1.0, ALU.max, ALU.add).then_inc(y_ready, 1)
                    dve.wait_ge(ey_ready, i * NT + t + 1)
                    dve.wait_ge(y_ready, i * NT + t + 1)
                    if t >= 1:
                        turned.await_filled(dve, i, t - 1)
                    dve.scalar_tensor_tensor(z[:], ey[:], 1.0, ry[:], ALU.min, ALU.add).then_inc(z_ready, 1)
                    if t >= 2:
                        add_product(i, t - 2)
                add_product(i, NT - 2)
                add_product(i, NT - 1)
            prod.await_emptied(dve, GH - 1, 2 * NT - 1)


def gat2_phase(p, h2):
    with Phase(p, "gat2") as f:
        core = GatCore(f, p, h2, D, [])
        bias = f.sb("bias", [TP, D])
        bias_in, x_in, biased, dve_step = f.sem("bias_in"), f.sem("x_in"), f.sem("biased"), f.sem("dve_step")
        agg = f.ring("agg", [3, 4, 5, 6, 7], ["dve"] * (2 * NT))
        block = f.block()

        @block.sync
        def _(sp):
            sp.dma_start(core.a_src[:], p.d["att_src2"].partition_broadcast(TP)).then_inc(core.vectors_in, 16)
            sp.dma_start(core.a_dst[:], p.d["att_dst2"].partition_broadcast(TP)).then_inc(core.vectors_in, 16)
            sp.dma_start(bias[:], p.d["b2"].partition_broadcast(TP)).then_inc(bias_in, 16)
            sp.dma_start(p.x[:], p.x_saved.rearrange("(t p) n -> p t n", p=TP)).then_inc(x_in, 16)

        @block.gpsimd
        def _(pool):
            pool.wait_ge(bias_in, 16)
            pool.wait_ge(x_in, 16)
            for t in range(NT):
                pool.tensor_tensor(p.x[:, t, :], p.x[:, t, :], bias[:], ALU.add).then_inc(biased, 1)
            pool.wait_ge(biased, NT)

        @block.tensor
        def _(pe):
            core.turn_maxima(pe, 0)
            core.spread_rows(pe, 0)
            for t in range(NT):
                if t % 2 == 0:
                    core.denominators(pe, 0, t // 2)
                for half in range(2):
                    u = 2 * t + half
                    agg.acquire(pe, 0, u)
                    for j in range(NT):
                        mm = pe.matmul(agg.bank(u)[0:TP, 0:HALF], core.e1[:, (t // 2) % 2, j, tile_cols(t % 2)],
                                       h2[:, j, half * HALF:(half + 1) * HALF], start=(j == 0), stop=(j == NT - 1))
                    mm.then_inc(agg.filled, 1)

        @block.scalar
        def _(act):
            core.misc.open(act, "act")
            core.empty_rows(act, 0)
            used = lambda eng, ch: eng.wait_ge(agg.filled, 4 * (ch - 1)) if ch >= 2 else None
            for ch in range(core.STEPS):
                for half in range(2):
                    core.exponentials(act, 0, ch, half, used)

        @block.vector
        def _(dve):
            step = Chain(dve, dve_step)
            core.misc.open(dve, "dve")
            core.den.open(dve, "dve")
            agg.open(dve, "dve")
            core.maxima(dve, step, 0, None)
            core.columns(dve, step, 0)
            for half in range(2):
                core.weights(dve, step, 0, 0, half)
            for t in range(NT):
                ch = t // 2 + 1
                if ch < core.STEPS:
                    core.weights(dve, step, 0, ch, t % 2)
                if t % 2 == 0:
                    core.reciprocals(dve, step, 0, t // 2)
                dve.wait_ge(biased, t + 1)
                for half in range(2):
                    u = 2 * t + half
                    agg.await_filled(dve, 0, u)
                    r = p.x[:, t, half * HALF:(half + 1) * HALF]
                    agg.give(dve.scalar_tensor_tensor(r, agg.bank(u)[0:TP, 0:HALF],
                                                      core.rden[:, t % 2:t % 2 + 1], r, ALU.mult, ALU.add), u)
            agg.await_emptied(dve, 0, 2 * NT - 1)



def tree_phase(p):
    with Phase(p, "tree") as f:
        w_in = f.sb("w_in", [128, KC, NODES])
        w_out = f.sb("w_out", [NODES, D])
        names = ("logits", "gelu", "right", "left", "visits", "coeff")
        logits, gelu, right, left, visits, coeff = (f.sb(s, [TP, NT, NODES]) for s in names)
        prod = f.sb("prod", [TP, NT, 10])
        sum4, sum5, n4, n5, late = (f.sb(s, [TP, NT]) for s in ("sum4", "sum5", "n4", "n5", "late"))
        coeffT = f.sb("coeffT", [NODES, NT, TP])
        weights_in, gelu_ready, logits_ready, coeff_ready, coeffT_ready, dve_step = (
            f.sem(s) for s in ("weights_in", "gelu_ready", "logits_ready", "coeff_ready", "coeffT_ready", "dve_step"))
        log = f.ring("log", [7], ["dve"])
        turned = f.ring("turned", [4, 5, 6], ["dve"] * 3)
        out = f.ring("out", [0, 1, 2, 3], ["dve"] * (2 * NT))
        block = f.block()

        @block.sync
        def _(sp):
            sp.dma_start(w_in[:], p.d["tree_in"].rearrange("p (k n) -> p k n", k=KC)).then_inc(weights_in, 16)
            sp.dma_start(w_out[:], p.d["tree_out"]).then_inc(weights_in, 16)

        @block.tensor
        def _(pe):
            pe.wait_ge(weights_in, 32)
            log.acquire(pe, 0, 0)
            for t in range(NT):
                for k in range(KC):
                    mm = pe.matmul(log.bank(0)[0:TP, t * NODES:(t + 1) * NODES], p.xT[:, k, tile_cols(t)],
                                   w_in[:, k, :], start=(k == 0), stop=(k == KC - 1))
            mm.then_inc(log.filled, 1)
            pe.wait_ge(coeff_ready, 1)
            for g, (t0, n) in enumerate(GROUPS):
                turned.acquire(pe, 0, g)
                for j in range(n):
                    mm = pe.transpose(turned.bank(g)[0:NODES, tile_cols(j)], coeff[:, t0 + j, :],
                                      p.ident[0:TP, 0:TP])
                mm.then_inc(turned.filled, 1)
            for t in range(NT):
                turned.await_emptied(pe, 0, next(g for g, (t0, n) in enumerate(GROUPS) if t < t0 + n))
                for half in range(2):
                    u = 2 * t + half
                    out.acquire(pe, 0, u)
                    pe.matmul(out.bank(u)[0:TP, 0:HALF], coeffT[:, t, :], w_out[:, half * HALF:(half + 1) * HALF],
                              start=True, stop=True).then_inc(out.filled, 1)

        @block.scalar
        def _(act):
            log.await_emptied(act, 0, 0)
            act.activation(gelu[:], logits[:], ACT.Gelu).then_inc(gelu_ready, 1)

        @block.vector
        def _(dve):
            step = Chain(dve, dve_step)
            for r in (log, turned, out):
                r.open(dve, "dve")
            step.add(dve.memset(visits[:, :, 0:1], 1.0))
            log.await_filled(dve, 0, 0)
            log.give(dve.tensor_copy(logits[:], log.bank(0)[0:TP, 0:NT * NODES].rearrange(
                "p (t n) -> p t n", t=NT)), 0)
            log.await_emptied(dve, 0, 0)
            step(dve.tensor_scalar(right[:], logits[:], 0.0, None, ALU.is_gt))
            step(dve.tensor_scalar(left[:], right[:], -1.0, 1.0, ALU.mult, ALU.add))
            for a, b in ((0, 1), (1, 3), (3, 7), (7, 10)):
                for first, way in ((1, left), (2, right)):
                    step.add(dve.tensor_tensor(visits[:, :, 2 * a + first:2 * (b - 1) + first + 1:2],
                                               visits[:, :, a:b], way[:, :, a:b], ALU.mult))
                step.wait()
            dve.wait_ge(gelu_ready, 1)
            step.add(dve.memset(coeff[:, :, 0:1], 0.0))
            for first in (1, 2):
                step.add(dve.tensor_tensor(coeff[:, :, first:18 + first + 1:2], visits[:, :, first:18 + first + 1:2],
                                           gelu[:, :, 0:10], ALU.mult))
            step(dve.tensor_tensor(prod[:], visits[:, :, 10:20], gelu[:, :, 10:20], ALU.mult))
            step.add(dve.tensor_reduce(sum4[:], prod[:], AX.X, ALU.add))
            step.add(dve.tensor_reduce(n5[:], visits[:, :, 15:20], AX.X, ALU.add))
            step.add(dve.tensor_reduce(n4[:], visits[:, :, 10:15], AX.X, ALU.add))
            step(dve.tensor_scalar(late[:], visits[:, :, 20], 6.0, None, ALU.mult))
            step(dve.scalar_tensor_tensor(late[:], n4[:], 6.0, late[:], ALU.mult, ALU.add))
            step(dve.scalar_tensor_tensor(late[:], n5[:], 5.0, late[:], ALU.mult, ALU.add))
            step(dve.tensor_tensor(sum5[:], late[:], gelu[:, :, 20], ALU.mult))
            step(dve.tensor_tensor(sum5[:], sum5[:], sum4[:], ALU.add))
            dve.tensor_tensor(coeff[:, :, 20], coeff[:, :, 20], sum5[:], ALU.add).then_inc(coeff_ready, 1)
            for g, (t0, n) in enumerate(GROUPS):
                turned.await_filled(dve, 0, g)
                turned.give(dve.tensor_copy(coeffT[:, t0:t0 + n, :], turned.bank(g)[0:NODES, 0:n * TP].rearrange(
                    "p (a b) -> p a b", a=n)), g)
            for t in range(NT):
                for half in range(2):
                    u = 2 * t + half
                    out.await_filled(dve, 0, u)
                    r = p.x[:, t, half * HALF:(half + 1) * HALF]
                    out.give(dve.tensor_tensor(r, out.bank(u)[0:TP, 0:HALF], r, ALU.add), u)
            out.await_emptied(dve, 0, 2 * NT - 1)



def gcn_phase(p):
    with Phase(p, "gcn") as f:
        w, b = f.sb("w", [128, KC, D]), f.sb("b", [TP, D])
        h = f.sb("h", [TP, NT, D])
        counts = f.sb("counts", [TP, 3, NT, TP])
        deg, root, dinv = f.sb("deg", [TP, NT]), f.sb("root", [TP, NT]), f.sb("dinv", [TP, NT])
        w_in, b_in, biased, counts_ready, root_ready, dinv_ready = (
            f.sem(s) for s in ("w_in", "b_in", "biased", "counts_ready", "root_ready", "dinv_ready"))
        degs = f.ring("degs", [7], ["dve"])
        prod = f.ring("prod", [0, 1, 2], ["act"] * (2 * NT))
        agg = f.ring("agg", [3, 4, 5, 6], ["dve"] * (2 * NT))
        block = f.block()
        halves = [(t, half) for t in range(NT) for half in range(2)]

        @block.sync
        def _(sp):
            sp.dma_start(w[:], p.d["gcn_w"].rearrange("p (k n) -> p k n", k=KC)).then_inc(w_in, 16)
            sp.dma_start(b[:], p.d["gcn_b"].partition_broadcast(TP)).then_inc(b_in, 16)

        def convert(eng, m, used):
            if used:
                eng.wait_ge(*used)
            t = m % NT
            eng.tensor_copy(counts[:, m % 3, :, :], p.AT[:, :, tile_cols(t)]).then_inc(counts_ready, 1)

        counts_used = f.sem("counts_used")

        @block.gpsimd
        def _(pool):
            pool.wait_ge(b_in, 16)
            for t in range(NT):
                pool.tensor_tensor(p.x[:, t, :], p.x[:, t, :], b[:], ALU.add).then_inc(biased, 1)
            pool.wait_ge(biased, NT)

        @block.tensor
        def _(pe):
            degs.acquire(pe, 0, 0)
            for t in range(NT):
                pe.wait_ge(counts_ready, t + 1)
                for j in range(NT):
                    mm = pe.matmul(degs.bank(0)[0:TP, t:t + 1], counts[:, t % 3, j, :], p.ones[0:TP, 0:1],
                                   start=(j == 0), stop=(j == NT - 1))
                mm.then_inc(counts_used, 1)
            pe.wait_ge(w_in, 16)
            for u, (t, half) in enumerate(halves):
                prod.acquire(pe, 0, u)
                for k in range(KC):
                    mm = pe.matmul(prod.bank(u)[0:TP, 0:HALF], p.xT[:, k, tile_cols(t)],
                                   w[:, k, half * HALF:(half + 1) * HALF], start=(k == 0), stop=(k == KC - 1))
                mm.then_inc(prod.filled, 1)
            prod.await_emptied(pe, 0, 2 * NT - 1)
            for u, (t, half) in enumerate(halves):
                pe.wait_ge(counts_ready, NT + t + 1)
                agg.acquire(pe, 0, u)
                for j in range(NT):
                    mm = pe.matmul(agg.bank(u)[0:TP, 0:HALF], counts[:, (NT + t) % 3, j, :],
                                   h[:, j, half * HALF:(half + 1) * HALF], start=(j == 0), stop=(j == NT - 1))
                mm.then_inc(agg.filled, 1)

        @block.scalar
        def _(act):
            prod.open(act, "act")
            degs.await_emptied(act, 0, 0)
            act.activation(root[:], deg[:], ACT.Sqrt).then_inc(root_ready, 1)
            act.wait_ge(dinv_ready, 1)
            for u, (t, half) in enumerate(halves):
                prod.await_filled(act, 0, u)
                prod.give(act.mul(h[:, t, half * HALF:(half + 1) * HALF], prod.bank(u)[0:TP, 0:HALF],
                                  dinv[:, t:t + 1]), u)

        @block.vector
        def _(dve):
            for r in (degs, agg):
                r.open(dve, "dve")
            for m in range(NT):
                convert(dve, m, (counts_used, m - 2) if m >= 3 else None)
            dve.wait_ge(counts_used, NT)
            degs.give(dve.tensor_copy(deg[:], degs.bank(0)[0:TP, 0:NT]), 0)
            dve.wait_ge(root_ready, 1)
            dve.reciprocal(dinv[:], root[:]).then_inc(dinv_ready, 1)
            dve.wait_ge(dinv_ready, 1)
            for m in range(NT, NT + 3):
                convert(dve, m, None)
            for u, (t, half) in enumerate(halves):
                dve.wait_ge(biased, t + 1)
                agg.await_filled(dve, 0, u)
                r = p.x[:, t, half * HALF:(half + 1) * HALF]
                agg.give(dve.scalar_tensor_tensor(r, agg.bank(u)[0:TP, 0:HALF], dinv[:, t:t + 1], r,
                                                  ALU.mult, ALU.add), u)
                if half and t + 3 < NT:
                    convert(dve, NT + t + 3, None)
            agg.await_emptied(dve, 0, 2 * NT - 1)



def performer_phase(p, yT):
    norm, eps = float(DH) ** -0.25, 1e-4
    with Phase(p, "perf") as f:
        w = f.sb("w", [128, KC, 384])
        pT = f.sb("pT", [128, 2 * M])
        half_norm2 = f.sb("half_norm2", [128, 2])
        qkT = f.sb("qkT", [128, 2, N])
        squares = f.sb("squares", [128, 2, N])
        v1 = f.sb("v1", [TP, NT, 2, 66])
        kf = f.sb("kf", [TP, NT, 2 * M])
        qf = f.sb("qf", [TP, 2, 2 * M])
        qfT = f.sb("qfT", [128, NT, 4, TP])
        ctx_sum = f.sb("ctx_sum", [128, 4 * 65])
        dg = f.sb("dg", [TP, NT, 2, 2])
        kmax, kmax1, stab, nstab = f.sb("kmax", [TP, NT, 2]), f.sb("kmax1", [TP, 2]), f.sb("stab", [TP, 2]), f.sb("nstab", [TP, 2])
        kbias = f.sb("kbias", [TP, NT, 2])
        qmax, qbias = f.sb("qmax", [TP, NT, 2]), f.sb("qbias", [TP, NT, 2])
        rden = f.sb("rden", [TP, NT, 2])
        y = f.sb("y", [TP, NT, 128])
        w_in, p_in, made, kmax_ready, stab_ready, kbias_ready, qbias_ready = (
            f.sem(s) for s in ("w_in", "p_in", "made", "kmax_ready", "stab_ready", "kbias_ready", "qbias_ready"))
        kexp_ready, k_ready, qexp_ready, dve_step, act_step, pool_turns = (
            f.sem(s) for s in ("kexp_ready", "k_ready", "qexp_ready", "dve_step", "act_step", "pool_turns"))
        wide = f.ring("wide", [0, 1, 2], ["act"] * 9)
        turn = f.ring("turn", [3, 4], ["dve"] * (2 * NT))
        feat = f.ring("feat", [5, 6], ["act"] * (2 * NT))
        narrow = f.ring("narrow", [7], ["dve"] * (2 + NT))
        block = f.block()

        @block.sync
        def _(sp):
            sp.dma_start(pT[:], p.d["perf_proj"]).then_inc(p_in, 16)
            with sp.Fori(0, PAIRS) as i:
                sp.wait_ge(turn.filled, i * 2 * NT)
                sp.dma_start(w[:], p.d["qkv1"][bass.ds(i, 1), :, :]).then_inc(w_in, 16)

        @block.gpsimd
        def _(pool):
            pool.memset(v1[:], 1.0).then_inc(made, 1)
            pool.memset(half_norm2[:], 0.0).then_inc(made, 1)
            pool.wait_ge(made, 2)
            for h in range(2):
                pool.memset(half_norm2[h * DH:(h + 1) * DH, h:h + 1], 0.5 * norm * norm).then_inc(made, 1)
            pool.wait_ge(made, 4)
            with pool.Fori(0, PAIRS) as i:
                pool.wait_ge(kmax_ready, i + 1)
                pool.sem_inc(pool_turns, 1)
                pool.partition_all_reduce(stab[:], kmax1[:], TP, RMAX).then_inc(stab_ready, 1)
            pool.wait_ge(pool_turns, PAIRS)

        @block.tensor
        def _(pe):
            def project(i, u, which, t):
                feat.acquire(pe, i, u)
                pe.matmul(feat.bank(u)[0:TP, :], qkT[:, which, tile_cols(t)], pT[:],
                          start=True, stop=True).then_inc(feat.filled, 1)

            def turn_q(i, t):
                pe.wait_ge(qexp_ready, i * NT + t + 1)
                u = NT + t
                turn.acquire(pe, i, u)
                for c in range(4):
                    mm = pe.transpose(turn.bank(u)[:, tile_cols(c)], qf[:, t % 2, c * 128:(c + 1) * 128],
                                      p.ident[0:TP, 0:TP])
                mm.then_inc(turn.filled, 1)

            pe.wait_ge(made, 4)
            pe.wait_ge(p_in, 16)
            with pe.Fori(0, PAIRS) as i:
                pe.wait_ge(w_in, i * 16 + 16)
                for which in range(2):
                    for g, (t0, n) in enumerate(GROUPS):
                        wide.acquire(pe, i, 3 * which + g)
                        for c in range(KC):
                            mm = pe.matmul(wide.bank(g)[:, 0:n * TP], w[:, c, which * 128:(which + 1) * 128],
                                           p.xT[:, c, tile_cols(t0, n)], start=(c == 0), stop=(c == KC - 1))
                        mm.then_inc(wide.filled, 1)
                for t in range(NT):
                    turn.acquire(pe, i, t)
                    for c in range(KC):
                        mm = pe.matmul(turn.bank(t)[0:TP, 0:128], p.xT[:, c, tile_cols(t)], w[:, c, 256:384],
                                       start=(c == 0), stop=(c == KC - 1))
                    mm.then_inc(turn.filled, 1)
                wide.await_emptied(pe, i, 5)
                narrow.acquire(pe, i, 0)
                for t in range(NT):
                    for which in range(2):
                        c = 4 * t + 2 * which
                        mm = pe.matmul(narrow.bank(0)[0:TP, c:c + 2], squares[:, which, tile_cols(t)],
                                       half_norm2[:], start=True, stop=True)
                mm.then_inc(narrow.filled, 1)
                for t in range(NT):
                    project(i, t, 1, t)
                for t in range(NT + 1):
                    if t < NT:
                        project(i, NT + t, 0, t)
                    if t >= 1:
                        turn_q(i, t - 1)
                narrow.acquire(pe, i, 1)
                turn.await_emptied(pe, i, NT - 1)
                pe.wait_ge(k_ready, i * NT + NT)
                for c in range(4):
                    for t in range(NT):
                        mm = pe.matmul(narrow.bank(0)[:, c * 65:(c + 1) * 65], kf[:, t, c * 128:(c + 1) * 128],
                                       v1[:, t, c // 2, 0:65], start=(t == 0), stop=(t == NT - 1))
                mm.then_inc(narrow.filled, 1)
                turn.await_emptied(pe, i, 2 * NT - 1)
                for t in range(NT):
                    narrow.acquire(pe, i, 2 + t)
                    for c in range(4):
                        mm = pe.matmul(narrow.bank(0)[0:TP, (c // 2) * 65:(c // 2 + 1) * 65], qfT[:, t, c, :],
                                       ctx_sum[:, c * 65:(c + 1) * 65], start=(c % 2 == 0), stop=(c % 2 == 1))
                    mm.then_inc(narrow.filled, 1)
                for g, (t0, n) in enumerate(GROUPS):
                    narrow.await_emptied(pe, i, 2 + t0 + n - 1)
                    wide.acquire(pe, i, 6 + g)
                    for j in range(n):
                        mm = pe.transpose(wide.bank(g)[:, tile_cols(j)], y[:, t0 + j, :], p.ident[0:TP, 0:TP])
                    mm.then_inc(wide.filled, 1)

        @block.scalar
        def _(act):
            for r in (wide, feat):
                r.open(act, "act")

            def exp_k(i, t):
                for h in range(2):
                    cols = slice(h * M, (h + 1) * M)
                    ins = act.activation(kf[:, t, cols], kf[:, t, cols], ACT.Exp, bias=kbias[:, t, h:h + 1], scale=norm)
                ins.then_inc(kexp_ready, 1)

            with act.Fori(0, PAIRS) as i:
                for which in range(2):
                    for g, (t0, n) in enumerate(GROUPS):
                        wide.await_filled(act, i, 3 * which + g)
                        cols = tile_cols(t0, n)
                        act.activation(squares[:, which, cols], wide.bank(g)[:, 0:n * TP], ACT.Square)
                        wide.give(act.copy(qkT[:, which, cols], wide.bank(g)[:, 0:n * TP]), 3 * which + g)
                for t in range(NT):
                    feat.await_filled(act, i, t)
                    feat.give(act.copy(kf[:, t, :], feat.bank(t)[0:TP, :]), t)
                for t in range(NT):
                    act.wait_ge(qbias_ready, i * NT + t + 1)
                    if t >= 2:
                        turn.await_filled(act, i, NT + t - 2)
                    act.activation(qf[:, t % 2, 0:M], feat.bank(t)[0:TP, 0:M], ACT.Exp,
                                   bias=qbias[:, t, 0:1], scale=norm)
                    act.activation(qf[:, t % 2, M:2 * M], feat.bank(t)[0:TP, M:2 * M], ACT.Exp,
                                   bias=qbias[:, t, 1:2], scale=norm).then_inc(qexp_ready, 1)
                    act.sem_inc(act_step, 1)
                    act.wait_ge(qexp_ready, i * NT + t + 1)
                    act.sem_inc(feat.emptied["act"], 1)
                    if t == 1:
                        act.wait_ge(kbias_ready, i + 1)
                    if t >= 2:
                        exp_k(i, t - 2)
                exp_k(i, NT - 2)
                exp_k(i, NT - 1)
                for g, (t0, n) in enumerate(GROUPS):
                    wide.await_filled(act, i, 6 + g)
                    wide.give(act.copy(yT[:, bass.ds(i, 1), tile_cols(t0, n)], wide.bank(g)[:, 0:n * TP]), 6 + g)
            wide.await_emptied(act, PAIRS - 1, 8)
            act.wait_ge(act_step, PAIRS * NT)
            feat.await_emptied(act, PAIRS - 1, 2 * NT - 1)

        @block.vector
        def _(dve):
            step = Chain(dve, dve_step)
            for r in (turn, narrow):
                r.open(dve, "dve")
            dve.wait_ge(made, 4)

            def empty_turned(i, t):
                u = NT + t
                turn.await_filled(dve, i, u)
                turn.give(dve.tensor_scalar(qfT[:, t, :, :].rearrange("p a b -> p (a b)"), turn.bank(u)[:, 0:4 * TP],
                                            eps, None, ALU.add), u)

            def finish_k(i, t):
                dve.wait_ge(kexp_ready, i * NT + t + 1)
                dve.tensor_scalar(kf[:, t, :], kf[:, t, :], eps, None, ALU.add).then_inc(k_ready, 1)

            with dve.Fori(0, PAIRS) as i:
                step.restart()
                for t in range(NT):
                    turn.await_filled(dve, i, t)
                    turn.give(dve.tensor_copy(v1[:, t, :, 0:DH], turn.bank(t)[0:TP, 0:128].rearrange(
                        "p (h e) -> p h e", h=2)), t)
                narrow.await_filled(dve, i, 0)
                narrow.give(dve.tensor_copy(dg[:].rearrange("p a b c -> p (a b c)"), narrow.bank(0)[0:TP, 0:4 * NT]), 0)
                for t in range(NT):
                    feat.await_emptied(dve, i, t)
                    step.add(dve.tensor_reduce(kmax[:, t, :], kf[:, t, :].rearrange("p (h m) -> p h m", h=2),
                                               AX.X, ALU.max))
                step.wait()
                dve.tensor_reduce(kmax1[:], kmax[:].rearrange("p t h -> p h t"), AX.X, ALU.max).then_inc(kmax_ready, 1)
                for t in range(NT):
                    feat.await_filled(dve, i, NT + t)
                    step(dve.tensor_reduce(qmax[:, t, :], feat.bank(t)[0:TP, :].rearrange("p (h m) -> p h m", h=2),
                                           AX.X, ALU.max))
                    dve.scalar_tensor_tensor(qbias[:, t, :], qmax[:, t, :], -norm, dg[:, t, 0, :],
                                             ALU.mult, ALU.subtract).then_inc(qbias_ready, 1)
                    if t == 1:
                        dve.wait_ge(stab_ready, i + 1)
                        step(dve.tensor_scalar(nstab[:], stab[:], -norm, None, ALU.mult))
                        step.add(dve.tensor_scalar(kbias[:, :, 0], dg[:, :, 1, 0], -1.0, nstab[:, 0:1],
                                                   ALU.mult, ALU.add))
                        dve.tensor_scalar(kbias[:, :, 1], dg[:, :, 1, 1], -1.0, nstab[:, 1:2],
                                          ALU.mult, ALU.add).then_inc(kbias_ready, 1)
                    if t >= 1:
                        empty_turned(i, t - 1)
                    if t >= 3:
                        finish_k(i, t - 3)
                empty_turned(i, NT - 1)
                for t in range(NT - 3, NT):
                    finish_k(i, t)
                narrow.await_filled(dve, i, 1)
                narrow.give(dve.tensor_copy(ctx_sum[:], narrow.bank(0)[:, 0:4 * 65]), 1)
                for t in range(NT):
                    narrow.await_filled(dve, i, 2 + t)
                    o = narrow.bank(0)[0:TP, 0:130].rearrange("p (h e) -> p h e", h=2)
                    step(dve.reciprocal(rden[:, t, :], o[:, :, DH]))
                    narrow.give(dve.tensor_tensor(y[:, t, :].rearrange("p (h e) -> p h e", h=2), o[:, :, 0:DH],
                                                  rden[:, t, :].unsqueeze(2).to_broadcast([TP, 2, DH]), ALU.mult),
                                2 + t)



def causal_attention_phase(p, yT):
    scale = float(DH) ** -0.5
    with Phase(p, "causal") as f:
        w = f.sb("w", [128, KC, 384])
        qkT = f.sb("qkT", [128, 2, N])
        v = f.sb("v", [TP, NT, 128])
        mask = f.sb("mask", [TP, TP])
        probs = f.sb("probs", [TP, 2, N])
        pT = f.sb("pT", [TP, 2, NT, TP])
        top, ntop, total, rtotal = (f.sb(s, [TP, 2 * NT]) for s in ("top", "ntop", "total", "rtotal"))
        y = f.sb("y", [TP, NT, 128])
        w_in, made, scores_ready, ntop_ready, probs_ready = (
            f.sem(s) for s in ("w_in", "made", "scores_ready", "ntop_ready", "probs_ready"))
        turned_low, turned_high, taken_low, taken_high = (
            f.sem(s) for s in ("turned_low", "turned_high", "taken_low", "taken_high"))
        wide_filled, wide_emptied, y_turned, y_taken, dve_step = (
            f.sem(s) for s in ("wide_filled", "wide_emptied", "y_turned", "y_taken", "dve_step"))
        narrow = f.ring("narrow", [6, 7], ["dve"] * (3 * NT))
        sets = [p.psA, p.psB]
        heads = [slice(h * DH, (h + 1) * DH) for h in range(2)]
        STEPS = 2 * NT
        high_blocks = [[b for b in (1, 2) if 4 * b <= s % NT] for s in range(STEPS)]
        high_count = [sum(len(x) for x in high_blocks[:s + 1]) for s in range(STEPS)]
        HIGH = high_count[-1]
        block = f.block()

        @block.sync
        def _(sp):
            with sp.Fori(0, PAIRS) as i:
                sp.wait_ge(narrow.filled, i * 3 * NT)
                sp.dma_start(w[:], p.d["qkv2"][bass.ds(i, 1), :, :]).then_inc(w_in, 16)

        @block.gpsimd
        def _(pool):
            pool.memset(mask[:], 0.0).then_inc(made, 1)
            pool.wait_ge(made, 1)
            pool.affine_select(out=mask[:], in_=mask[:], compare_op=ALU.is_ge, fill=-1e30, base=0,
                               pattern=[[-1, TP]], channel_multiplier=1).then_inc(made, 1)

        def scores(s):
            return sets[s % 2][0:TP, :, :].rearrange("p a b -> p (a b)")

        @block.tensor
        def _(pe):
            def score(i, s):
                h, t = divmod(s, NT)
                n = (t + 1) * TP
                if s >= 2:
                    pe.wait_ge(taken_low, i * STEPS + s - 1)
                    pe.wait_ge(taken_high, i * HIGH + high_count[s - 2])
                for a in range(0, n, 512):
                    b = min(n, a + 512)
                    mm = pe.matmul(scores(s)[:, a:b], qkT[heads[h], 0, tile_cols(t)], qkT[heads[h], 1, a:b],
                                   start=True, stop=True)
                mm.then_inc(scores_ready, 1)

            def turn(i, s):
                t = s % NT
                pe.wait_ge(probs_ready, i * STEPS + s + 1)
                for b in range(3):
                    js = range(4 * b, min(4 * b + 4, t + 1))
                    for j in js:
                        mm = pe.transpose(sets[s % 2][0:TP, b, tile_cols(j - 4 * b)], probs[:, s % 2, tile_cols(j)],
                                          p.ident[0:TP, 0:TP])
                    if js:
                        mm.then_inc(turned_low if b == 0 else turned_high, 1)

            def attend(i, s):
                h, t = divmod(s, NT)
                pe.wait_ge(taken_low, i * STEPS + s + 1)
                pe.wait_ge(taken_high, i * HIGH + high_count[s])
                u = NT + s
                narrow.acquire(pe, i, u)
                for j in range(t + 1):
                    mm = pe.matmul(narrow.bank(u)[0:TP, 0:DH], pT[:, s % 2, j, :], v[:, j, heads[h]],
                                   start=(j == 0), stop=(j == t))
                mm.then_inc(narrow.filled, 1)

            pe.wait_ge(made, 2)
            with pe.Fori(0, PAIRS) as i:
                pe.wait_ge(w_in, i * 16 + 16)
                pe.wait_ge(y_taken, i * 3)
                pe.wait_ge(taken_low, i * STEPS)
                pe.wait_ge(taken_high, i * HIGH)
                for which in range(2):
                    for g, (t0, n) in enumerate(GROUPS):
                        for c in range(KC):
                            mm = pe.matmul(sets[which][:, g, 0:n * TP], w[:, c, which * 128:(which + 1) * 128],
                                           p.xT[:, c, tile_cols(t0, n)], start=(c == 0), stop=(c == KC - 1))
                        mm.then_inc(wide_filled, 1)
                for t in range(NT):
                    narrow.acquire(pe, i, t)
                    for c in range(KC):
                        mm = pe.matmul(narrow.bank(t)[0:TP, 0:128], p.xT[:, c, tile_cols(t)], w[:, c, 256:384],
                                       start=(c == 0), stop=(c == KC - 1))
                    mm.then_inc(narrow.filled, 1)
                pe.wait_ge(wide_emptied, i * 6 + 6)
                narrow.await_emptied(pe, i, NT - 1)
                score(i, 0)
                for s in range(STEPS + 1):
                    if s + 1 < STEPS:
                        score(i, s + 1)
                    if s < STEPS:
                        turn(i, s)
                    if s >= 1:
                        attend(i, s - 1)
                for g, (t0, n) in enumerate(GROUPS):
                    narrow.await_emptied(pe, i, NT + NT + t0 + n - 1)
                    for j in range(n):
                        mm = pe.transpose(sets[0][:, g, tile_cols(j)], y[:, t0 + j, :], p.ident[0:TP, 0:TP])
                    mm.then_inc(y_turned, 1)

        @block.scalar
        def _(act):
            def take_high(i, s):
                before = high_count[s] - len(high_blocks[s])
                for k, b in enumerate(high_blocks[s]):
                    n = min(4 * b + 4, s % NT + 1) - 4 * b
                    act.wait_ge(turned_high, i * HIGH + before + k + 1)
                    act.copy(pT[:, s % 2, 4 * b:4 * b + n, :], sets[s % 2][0:TP, b, 0:n * TP].rearrange(
                        "p (a b) -> p a b", a=n)).then_inc(taken_high, 1)

            with act.Fori(0, PAIRS) as i:
                for which in range(2):
                    for g, (t0, n) in enumerate(GROUPS):
                        act.wait_ge(wide_filled, i * 6 + 3 * which + g + 1)
                        act.copy(qkT[:, which, tile_cols(t0, n)], sets[which][:, g, 0:n * TP]).then_inc(wide_emptied, 1)
                for s in range(STEPS):
                    n = (s % NT + 1) * TP
                    act.wait_ge(ntop_ready, i * STEPS + s + 1)
                    act.activation(probs[:, s % 2, 0:n], scores(s)[:, 0:n], ACT.Exp, bias=ntop[:, s:s + 1],
                                   scale=scale, accum_out=total[:, s:s + 1]).then_inc(probs_ready, 1)
                    if s >= 1:
                        take_high(i, s - 1)
                take_high(i, STEPS - 1)
                for g, (t0, n) in enumerate(GROUPS):
                    act.wait_ge(y_turned, i * 3 + g + 1)
                    act.copy(yT[:, bass.ds(i, 1), tile_cols(t0, n)], sets[0][:, g, 0:n * TP]).then_inc(y_taken, 1)
            act.wait_ge(y_taken, PAIRS * 3)

        @block.vector
        def _(dve):
            step = Chain(dve, dve_step)
            narrow.open(dve, "dve")
            dve.wait_ge(made, 2)

            def take_low(i, s):
                n = min(4, s % NT + 1)
                dve.wait_ge(turned_low, i * STEPS + s + 1)
                dve.tensor_copy(pT[:, s % 2, 0:n, :], sets[s % 2][0:TP, 0, 0:n * TP].rearrange(
                    "p (a b) -> p a b", a=n)).then_inc(taken_low, 1)

            def finish(i, s):
                h, t = divmod(s, NT)
                step(dve.reciprocal(rtotal[:, s:s + 1], total[:, s:s + 1]))
                narrow.await_filled(dve, i, NT + s)
                narrow.give(dve.tensor_scalar(y[:, t, heads[h]], narrow.bank(NT + s)[0:TP, 0:DH],
                                              rtotal[:, s:s + 1], None, ALU.mult), NT + s)

            with dve.Fori(0, PAIRS) as i:
                step.restart()
                for t in range(NT):
                    narrow.await_filled(dve, i, t)
                    narrow.give(dve.tensor_copy(v[:, t, :], narrow.bank(t)[0:TP, 0:128]), t)
                for s in range(STEPS):
                    t = s % NT
                    n = (t + 1) * TP
                    dve.wait_ge(scores_ready, i * STEPS + s + 1)
                    own = scores(s)[:, tile_cols(t)]
                    step(dve.tensor_tensor(own, own, mask[:], ALU.add))
                    step(dve.tensor_reduce(top[:, s:s + 1], scores(s)[:, 0:n], AX.X, ALU.max))
                    dve.tensor_scalar(ntop[:, s:s + 1], top[:, s:s + 1], -scale, None,
                                      ALU.mult).then_inc(ntop_ready, 1)
                    if s >= 1:
                        take_low(i, s - 1)
                    if s >= 2:
                        finish(i, s - 2)
                take_low(i, STEPS - 1)
                finish(i, STEPS - 2)
                finish(i, STEPS - 1)



def routing_phase(p, xn, xbuf, dest, gate):
    with Phase(p, "route") as f:
        wg = f.sb("wg", [128, KC, E])
        zeros = f.sb("zeros", [CT, D])
        iota_i, node_i = f.sb("iota_i", [TP, E], I32), f.sb("node_i", [TP, NT], I32)
        iota, node = f.sb("iota", [TP, E]), f.sb("node", [TP, NT])
        before = f.sb("before", [TP, TP])
        wide = lambda s: f.sb(s, [TP, NT, E])
        logits, rest, cand = wide("logits"), wide("rest"), wide("cand")
        hot = [wide("hot0"), wide("hot1")]
        count, earlier, pos = wide("count"), wide("earlier"), wide("pos")
        col = lambda s: f.sb(s, [TP, NT])
        best, index = [col("best0"), col("best1")], [col("index0"), col("index1")]
        gap, ratio, den, gates = col("gap"), col("ratio"), col("den"), [col("gates0"), col("gates1")]
        slot, valid, row, trash, tmp = col("slot"), col("valid"), col("row"), col("trash"), col("tmp")
        w_in, made, zeroed, gap_ready, ratio_ready, counted, dest_ready, scattered, dve_step, waited = (
            f.sem(s) for s in ("w_in", "made", "zeroed", "gap_ready", "ratio_ready", "counted", "dest_ready",
                               "scattered", "dve_step", "waited"))
        log = f.ring("log", [0], ["dve"])
        sums = f.ring("sums", [1], ["dve"])
        block = f.block()
        bcast = lambda a: a[:].unsqueeze(2).to_broadcast([TP, NT, E])
        each = lambda a: a[:].unsqueeze(1).to_broadcast([TP, NT, E])

        @block.sync
        def _(sp):
            sp.dma_start(wg[:], p.d["gate_w"].rearrange("p (k n) -> p k n", k=KC)).then_inc(w_in, 16)
            sp.wait_ge(made, 4)
            for k in range(TRASH // CT):
                sp.dma_start(xbuf[k * CT:(k + 1) * CT, :], zeros[:]).then_inc(zeroed, 16)
            sp.wait_ge(zeroed, 16 * (TRASH // CT))

        @block.gpsimd
        def _(pool):
            pool.memset(zeros[:], 0.0).then_inc(made, 1)
            pool.iota(iota_i[:], [[1, E]], base=0, channel_multiplier=0).then_inc(made, 1)
            pool.iota(node_i[:], [[TP, NT]], base=0, channel_multiplier=1).then_inc(made, 1)
            pool.memset(before[:], 1.0).then_inc(made, 1)
            pool.wait_ge(made, 4)
            pool.affine_select(out=before[:], in_=before[:], compare_op=ALU.is_gt, fill=0.0, base=0,
                               pattern=[[1, TP]], channel_multiplier=-1).then_inc(made, 1)
            pool.wait_ge(zeroed, 16 * (TRASH // CT))
            for c in range(2):
                pool.wait_ge(dest_ready, c + 1)
                for t in range(NT):
                    pool.indirect_dma_start(
                        xbuf[:, :], bass.IndirectOffsetOnAxis(ap=dest[:, c, 0, t:t + 1], axis=0),
                        xn[:, t, :], None).then_inc(scattered, 16)
            pool.wait_ge(scattered, 16 * 2 * NT)

        @block.tensor
        def _(pe):
            pe.wait_ge(w_in, 16)
            pe.wait_ge(made, 5)
            log.acquire(pe, 0, 0)
            for t in range(NT):
                for k in range(KC):
                    mm = pe.matmul(log.bank(0)[0:TP, t * E:(t + 1) * E], p.xT[:, k, tile_cols(t)], wg[:, k, :],
                                   start=(k == 0), stop=(k == KC - 1))
            mm.then_inc(log.filled, 1)
            pe.wait_ge(counted, 1)
            sums.acquire(pe, 0, 0)
            for t in range(NT):
                o = sums.bank(0)[0:TP, t * E:(t + 1) * E]
                pe.matmul(o, before[:], count[:, t, :], start=True, stop=False)
                mm = pe.matmul(o, p.ones[0:TP, 0:TP], earlier[:, t, :], start=False, stop=True)
            mm.then_inc(sums.filled, 1)

        @block.scalar
        def _(act):
            act.wait_ge(gap_ready, 1)
            act.activation(ratio[:], gap[:], ACT.Exp).then_inc(ratio_ready, 1)

        @block.vector
        def _(dve):
            step = Chain(dve, dve_step)
            log.open(dve, "dve")
            sums.open(dve, "dve")
            dve.wait_ge(made, 5)
            step.add(dve.tensor_copy(iota[:], iota_i[:]))
            step.add(dve.tensor_copy(node[:], node_i[:]))
            log.await_filled(dve, 0, 0)
            log.give(dve.tensor_copy(logits[:], log.bank(0)[0:TP, 0:NT * E].rearrange("p (t e) -> p t e", t=NT)), 0)
            log.await_emptied(dve, 0, 0)
            step.wait()
            for c, x in enumerate((logits, rest)):
                step(dve.tensor_reduce(best[c][:], x[:], AX.X, ALU.max))
                step(dve.tensor_tensor(cand[:], x[:], bcast(best[c]), ALU.is_lt))
                step(dve.scalar_tensor_tensor(cand[:].rearrange("p t e -> p (t e)"), cand[:].rearrange("p t e -> p (t e)"),
                                              float(E), cand[:].rearrange("p t e -> p (t e)"), ALU.mult, ALU.max))
                step(dve.tensor_tensor(cand[:], cand[:], each(iota), ALU.add))
                step(dve.tensor_reduce(index[c][:], cand[:], AX.X, ALU.min))
                step(dve.tensor_tensor(hot[c][:], each(iota), bcast(index[c]), ALU.is_equal))
                if c == 0:
                    step(dve.scalar_tensor_tensor(rest[:].rearrange("p t e -> p (t e)"), hot[0][:].rearrange("p t e -> p (t e)"),
                                                  NEG, logits[:].rearrange("p t e -> p (t e)"), ALU.mult, ALU.add))
            dve.tensor_tensor(gap[:], best[1][:], best[0][:], ALU.subtract).then_inc(gap_ready, 1)
            step(dve.tensor_tensor(count[:], hot[0][:], hot[1][:], ALU.add))
            step(dve.memset(earlier[:, 0, :], 0.0))
            for t in range(1, NT):
                ins = dve.tensor_tensor(earlier[:, t, :], earlier[:, t - 1, :], count[:, t - 1, :], ALU.add)
                if t < NT - 1:
                    step(ins)
                else:
                    ins.then_inc(counted, 1)
            dve.wait_ge(ratio_ready, 1)
            step(dve.tensor_scalar(den[:], ratio[:], 1.0, None, ALU.add))
            step(dve.reciprocal(gates[0][:], den[:]))
            step(dve.tensor_tensor(gates[1][:], gates[0][:], ratio[:], ALU.mult))
            sums.await_filled(dve, 0, 0)
            sums.give(dve.tensor_copy(pos[:], sums.bank(0)[0:TP, 0:NT * E].rearrange("p (t e) -> p t e", t=NT)), 0)
            sums.await_emptied(dve, 0, 0)
            for c in range(2):
                step(dve.tensor_tensor(cand[:], pos[:], hot[c][:], ALU.mult))
                step(dve.tensor_reduce(slot[:], cand[:], AX.X, ALU.add))
                step(dve.tensor_scalar(valid[:], slot[:], float(CAP), None, ALU.is_lt))
                step(dve.scalar_tensor_tensor(row[:], index[c][:], float(CAP), slot[:], ALU.mult, ALU.add))
                step(dve.tensor_scalar(trash[:], node[:], 2.0, float(TRASH + c), ALU.mult, ALU.add))
                step(dve.tensor_tensor(tmp[:], row[:], trash[:], ALU.subtract))
                step(dve.tensor_tensor(tmp[:], tmp[:], valid[:], ALU.mult))
                step(dve.tensor_tensor(tmp[:], tmp[:], trash[:], ALU.add))
                step(dve.tensor_tensor(row[:], row[:], valid[:], ALU.mult))
                step(dve.tensor_tensor(gate[:, c, :], gates[c][:], valid[:], ALU.mult))
                step(dve.tensor_copy(dest[:, c, 1, :], row[:]))
                dve.tensor_copy(dest[:, c, 0, :], tmp[:]).then_inc(dest_ready, 1)
                dve.wait_ge(dest_ready, c + 1)


def experts_phase(p, xbuf, ybuf):
    with Phase(p, "experts") as f:
        HT = HID // HC // 128
        WS = 3
        x = f.sb("x", [CT, 3, D])
        xT = f.sb("xT", [128, KC, CAP])
        fc = f.sb("fc", [128, WS, KC, 512])
        pr = f.sb("pr", [128, WS, HT, D])
        hT = f.sb("hT", [128, 2, HT, CAP])
        yT = f.sb("yT", [128, KC, CAP])
        y = f.sb("y", [CT, 3, D])
        x_in, y_out, yT_ready = f.sem("x_in"), f.sem("y_out"), f.sem("yT_ready")
        fc_in = [f.sem(f"fc_in{k}") for k in range(WS)]
        pr_in = [f.sem(f"pr_in{k}") for k in range(WS)]
        work = f.ring("work", [6, 7], ["dve"] * KC + ["act"] * (HC * HT) + ["dve"] * 6)
        FIRST_H, FIRST_Y = KC, KC + HC * HT
        projected, outs_emptied = f.sem("projected"), f.sem("outs_emptied")
        block = f.block()

        @block.sync
        def _(sp):
            with sp.Fori(0, E) as e:
                sp.wait_ge(work.filled, e * work.n)
                sp.dma_start(x[:], xbuf[bass.ds(e * CAP, CAP), :].rearrange("(a p) n -> p a n", p=CT)
                             ).then_inc(x_in, 16)
                for c in range(HC):
                    k = c % WS
                    sp.wait_ge(work.emptied["act"], (e * HC + c - WS + 1 + HC) * HT)
                    sp.dma_start(fc[:, k, :, :], p.d["c_fc"][bass.ds(e * HC + c, 1), :, :]).then_inc(fc_in[k], 16)
                    sp.wait_ge(projected, e * HC + c + 1)
                    sp.dma_start(pr[:, k, :, :], p.d["c_proj_e"][bass.ds(e * HC + c, 1), :, :]).then_inc(pr_in[k], 16)

        @block.tensor
        def _(pe):
            pe.sem_inc(projected, WS)

            def hidden(e, c):
                k = c % WS
                pe.wait_ge(fc_in[k], (e * (HC // WS) + c // WS) * 16 + 16)
                for b in range(HT):
                    u = FIRST_H + c * HT + b
                    work.acquire(pe, e, u)
                    for q in range(KC):
                        mm = pe.matmul(work.bank(u)[:, 0:CAP], fc[:, k, q, b * 128:(b + 1) * 128], xT[:, q, :],
                                       start=(q == 0), stop=(q == KC - 1))
                    mm.then_inc(work.filled, 1)

            def project(e, c):
                k = c % WS
                pe.wait_ge(pr_in[k], (e * (HC // WS) + c // WS) * 16 + 16)
                if c == 0:
                    pe.wait_ge(outs_emptied, e * KC)
                for b in range(HT):
                    work.await_emptied(pe, e, FIRST_H + c * HT + b)
                    for q in range(KC):
                        mm = pe.matmul(p.bank[q][:, 0:CAP], pr[:, k, b, q * 128:(q + 1) * 128], hT[:, c % 2, b, :],
                                       start=(c == 0 and b == 0), stop=(c == HC - 1 and b == HT - 1))
                mm.then_inc(projected, 1)

            with pe.Fori(0, E) as e:
                pe.wait_ge(x_in, e * 16 + 16)
                for q in range(KC):
                    work.acquire(pe, e, q)
                    for a in range(3):
                        mm = pe.transpose(work.bank(q)[:, a * CT:(a + 1) * CT], x[:, a, q * 128:(q + 1) * 128],
                                          p.ident[0:CT, 0:CT])
                    mm.then_inc(work.filled, 1)
                work.await_emptied(pe, e, KC - 1)
                hidden(e, 0)
                for c in range(HC):
                    if c + 1 < HC:
                        hidden(e, c + 1)
                    project(e, c)
                for a in range(3):
                    for half in range(2):
                        u = FIRST_Y + 2 * a + half
                        work.acquire(pe, e, u)
                        for q in range(3):
                            k = 3 * half + q
                            pe.wait_ge(outs_emptied, e * KC + k + 1)
                            mm = pe.transpose(work.bank(u)[0:CT, q * 128:(q + 1) * 128], yT[:, k, a * CT:(a + 1) * CT],
                                              p.ident[:])
                        mm.then_inc(work.filled, 1)

        @block.scalar
        def _(act):
            work.open(act, "act")
            with act.Fori(0, E) as e:
                for c in range(HC):
                    if c >= 2:
                        act.wait_ge(projected, e * HC + c - 1 + WS)
                    for b in range(HT):
                        u = FIRST_H + c * HT + b
                        work.await_filled(act, e, u)
                        work.give(act.activation(hT[:, c % 2, b, :], work.bank(u)[:, 0:CAP], ACT.Gelu), u)
                for a in range(3):
                    work.await_emptied(act, e, FIRST_Y + 2 * a + 1)
                    act.dma_start(ybuf[bass.ds(e * CAP + a * CT, CT), :], y[:, a, :]).then_inc(y_out, 16)
            act.wait_ge(y_out, 16 * 3 * E)

        @block.vector
        def _(dve):
            work.open(dve, "dve")
            with dve.Fori(0, E) as e:
                for q in range(KC):
                    work.await_filled(dve, e, q)
                    work.give(dve.tensor_copy(xT[:, q, :], work.bank(q)[:, 0:CAP]), q)
                dve.wait_ge(projected, e * HC + HC + WS)
                for q in range(KC):
                    dve.tensor_copy(yT[:, q, :], p.bank[q][:, 0:CAP]).then_inc(outs_emptied, 1)
                dve.wait_ge(y_out, e * 48)
                for a in range(3):
                    for half in range(2):
                        u = FIRST_Y + 2 * a + half
                        work.await_filled(dve, e, u)
                        work.give(dve.tensor_copy(y[:, a, half * HALF:(half + 1) * HALF],
                                                  work.bank(u)[0:CT, 0:HALF]), u)


def combine_phase(p, ybuf, dest, gate, out):
    with Phase(p, "combine") as f:
        rows = f.sb("rows", [TP, 4, D])
        fetched = [f.sem(f"fetched{k}") for k in range(4)]
        summed, stored = f.sem("summed"), f.sem("stored")
        block = f.block()

        @block.gpsimd
        def _(pool):
            for n in range(2 * NT):
                t, c = divmod(n, 2)
                if n >= 4:
                    pool.wait_ge(summed, n - 3)
                pool.indirect_dma_start(
                    rows[:, n % 4, :], None, ybuf[:, :],
                    bass.IndirectOffsetOnAxis(ap=dest[:, c, 1, t:t + 1], axis=0)).then_inc(fetched[n % 4], 16)

        @block.vector
        def _(dve):
            for n in range(2 * NT):
                t, c = divmod(n, 2)
                dve.wait_ge(fetched[n % 4], 16 * (n // 4 + 1))
                dve.wait_ge(summed, n)
                dve.scalar_tensor_tensor(p.x[:, t, :], rows[:, n % 4, :], gate[:, c, t:t + 1], p.x[:, t, :],
                                         ALU.mult, ALU.add).then_inc(summed, 1)

        @block.sync
        def _(sp):
            for t in range(NT):
                sp.wait_ge(summed, 2 * t + 2)
                sp.dma_start(out[t * TP:(t + 1) * TP, :], p.x[:, t, :]).then_inc(stored, 16)
            sp.wait_ge(stored, 16 * NT)


def load_phase(p, of):
    with Phase(p, "load") as f:
        x_in = f.sem("x_in")
        block = f.block()

        @block.sync
        def _(sp):
            sp.dma_start(p.x[:], of.rearrange("(t p) n -> p t n", p=TP)).then_inc(x_in, 16)
            sp.wait_ge(x_in, 16)


def store_phase(p, to):
    with Phase(p, "store") as f:
        stored = f.sem("stored")
        block = f.block()

        @block.sync
        def _(sp):
            sp.dma_start(to.rearrange("(t p) n -> p t n", p=TP), p.x[:]).then_inc(stored, 16)
            sp.wait_ge(stored, 16)


def build(nc, d, out):
    with ExitStack() as ctx:
        p = Program(nc, ctx, d)
        p.x_saved = p.dram("x_saved", (N, D), F32)
        xbuf, ybuf = p.dram("xbuf", (SLOTS, D), F32), p.dram("ybuf", (TRASH, D), F32)
        setup_phase(p)

        def sb(c, name, shape, dt=F32):
            return c.enter_context(nc.sbuf_tensor(name, shape, dt))

        with ExitStack() as edges:
            p.AT = sb(edges, "AT", [TP, NT, N], U16)
            with ExitStack() as c0:
                h2 = sb(c0, "h2", [TP, NT, D])
                with ExitStack() as c1:
                    p.xT = sb(c1, "xT_0", [128, KC, N])
                    adjacency_phase(p)
                    with ExitStack() as c2:
                        p.x = sb(c2, "x_0", [TP, NT, D])
                        load_phase(p, d["x"])
                        with ExitStack() as c3:
                            xn = sb(c3, "xn_0", [TP, NT, D])
                            layer_norm_phase(p, "ln0", p.x, xn)
                        with ExitStack() as c3:
                            yT = sb(c3, "yT_0", [128, KC, N])
                            linear_attention_phase(p, yT)
                            projection_phase(p, "proj0", yT, "proj0", p.x, bias="proj0_b")
                        store_phase(p, p.x_saved)
                    gat1_phase(p, h2)
                with ExitStack() as c1:
                    p.x = sb(c1, "x_1", [TP, NT, D])
                    gat2_phase(p, h2)
                    store_phase(p, p.x_saved)
            p.x = sb(edges, "x_2", [TP, NT, D])
            load_phase(p, p.x_saved)
            with ExitStack() as c1:
                p.xT = sb(c1, "xT_1", [128, KC, N])
                with ExitStack() as c2:
                    xn = sb(c2, "xn_1", [TP, NT, D])
                    layer_norm_phase(p, "ln1", p.x, xn)
                tree_phase(p)
                with ExitStack() as c2:
                    xn = sb(c2, "xn_2", [TP, NT, D])
                    layer_norm_phase(p, "ln2", p.x, xn)
                gcn_phase(p)
                with ExitStack() as c2:
                    yT = sb(c2, "yT_1", [128, KC, N])
                    performer_phase(p, yT)
                    projection_phase(p, "proj1", yT, "proj1", p.x)
            store_phase(p, p.x_saved)
        with ExitStack() as c0:
            p.x = sb(c0, "x_3", [TP, NT, D])
            load_phase(p, p.x_saved)
            dest, gate = sb(c0, "dest", [TP, 2, 2, NT], I32), sb(c0, "gate", [TP, 2, NT])
            with ExitStack() as c1:
                z = sb(c1, "z", [TP, NT, D])
                p.xT = sb(c1, "xT_2", [128, KC, N])
                layer_norm_phase(p, "ln3", p.x, z, transposed=False)
                with ExitStack() as c2:
                    xn = sb(c2, "xn_3", [TP, NT, D])
                    layer_norm_phase(p, "ln4", z, xn, w_name="ln1_w", plain=sb(c2, "plain", [TP, 2, D]))
                with ExitStack() as c2:
                    yT = sb(c2, "yT_2", [128, KC, N])
                    causal_attention_phase(p, yT)
                    projection_phase(p, "proj2", yT, "proj2", z, also=p.x)
                with ExitStack() as c2:
                    layer_norm_phase(p, "ln5", z, z, w_name="ln2_w", plain=sb(c2, "plain2", [TP, 2, D]))
                routing_phase(p, z, xbuf, dest, gate)
            experts_phase(p, xbuf, ybuf)
            combine_phase(p, ybuf, dest, gate, out)


def blocks_of(w, n):
    k, m = w.shape
    return np.ascontiguousarray(w.reshape(k // 128, 128, m // n, n).transpose(2, 1, 0, 3)).reshape(m // n, 128, -1)


def pair_weights(q, k, v):
    w = np.stack([q, k, v]).reshape(3, KC, 128, PAIRS, 128)
    return np.ascontiguousarray(w.transpose(3, 2, 1, 0, 4)).reshape(PAIRS, 128, KC * 384)


def both_heads(w):
    out = np.zeros((2, DH, 2, w.shape[1]), w.dtype)
    out[0, :, 0], out[1, :, 1] = w, w
    return out.reshape(2 * DH, 2 * w.shape[1])


def kernel(**inputs):
    import concourse.bacc as bacc
    from concourse.bass_utils import run_bass_kernel_spmd as run

    a = {k: np.asarray(v) for k, v in inputs.items()}
    lay = {
        "x": a["x"],
        "src": a["src"].reshape(ET, TP).T,
        "dst": a["dst"].reshape(ET, TP).T,
        "qkv0": pair_weights(*(a["L0_mix_qkv_w"][n * D:(n + 1) * D].T for n in range(3))),
        "proj0": blocks_of(a["L0_mix_proj_w"].T, D)[0],
        "tree_in": blocks_of(a["L0_ffn_weights_in"].T, NODES)[0],
        "tree_out": a["L0_ffn_weights_out"],
        "gcn_w": blocks_of(a["L1_gnn_W"], D)[0],
        "gcn_b": a["L1_gnn_b"].reshape(1, D),
        "qkv1": pair_weights(a["L1_mix_Wq"], a["L1_mix_Wk"], a["L1_mix_Wv"]),
        "perf_proj": both_heads(a["L1_mix_proj"].T),
        "proj1": blocks_of(a["L1_mix_Wo"], D)[0],
        "ln1_w": a["L1_ffn_ln1_w"].reshape(1, D),
        "ln2_w": a["L1_ffn_ln2_w"].reshape(1, D),
        "qkv2": pair_weights(*(a["L1_ffn_c_attn_w"][n * D:(n + 1) * D].T for n in range(3))),
        "proj2": blocks_of(a["L1_ffn_c_proj_w"].T, D)[0],
        "gate_w": blocks_of(a["L1_ffn_w_g"].T, E)[0],
        "c_fc": np.concatenate([blocks_of(w, HID // HC) for w in a["L1_ffn_c_fc"]]),
        "c_proj_e": np.concatenate([blocks_of(w, D) for w in a["L1_ffn_c_proj_e"].reshape(E * HC, HID // HC, D)]),
        "W1": blocks_of(a["L0_gnn_W1"], GD),
        "att_src1": a["L0_gnn_att_src1"],
        "att_dst1": a["L0_gnn_att_dst1"],
        "b1": a["L0_gnn_b1"].reshape(GH, GD),
        "W2": np.stack([blocks_of(w, D)[0] for w in a["L0_gnn_W2"].reshape(GH, GD, D)]),
        "att_src2": a["L0_gnn_att_src2"],
        "att_dst2": a["L0_gnn_att_dst2"],
        "b2": a["L0_gnn_b2"].reshape(1, D),
        "proj0_b": a["L0_mix_proj_b"].reshape(1, D),
    }
    lay = {k: np.ascontiguousarray(v) for k, v in lay.items()}
    nc = bacc.Bacc("TRN2", target_bir_lowering=False, num_devices=1)
    d = {k: nc.dram_tensor("in_" + k, v.shape, mybir.dt.from_np(v.dtype), kind="ExternalInput").ap() for k, v in lay.items()}
    out = nc.dram_tensor("out", (N, D), F32, kind="ExternalOutput").ap()
    build(nc, d, out)
    r = run(nc, [{"in_" + k: v for k, v in lay.items()}], core_ids=[0])
    return r.results[0]["out"]
```
